# Optimizing a Trainium2 kernel written in Bass

```python
import numpy as np
import jax
import jax.numpy as jnp

def _softmax(x, axis=-1):
    return jax.nn.softmax(x, axis=axis)

def _gelu(x):
    return jax.nn.gelu(x, approximate=True)

def _silu(x):
    return jax.nn.silu(x)

def _sigmoid(x):
    return jax.nn.sigmoid(x)

def _layernorm(x, axis=-1, eps=1e-05):
    m = jnp.mean(x, axis=axis, keepdims=True)
    v = jnp.var(x, axis=axis, keepdims=True)
    return (x - m) / jnp.sqrt(v + eps)

def _scatter_add(tgt, idx, src, axis=0):
    return tgt.at[idx].add(src)

def _segment_sum(src, seg, n):
    return jax.ops.segment_sum(src, seg, n)
kernel_name = 'mk_adj_resnorm_d2_adj_r2_ce7e87'

def setup_inputs(seed: int=0):
    np.random.seed(seed)
    _w = jnp.asarray

    def _rec_inputs():
        import jax
        import jax.numpy as jnp
        _gk = jax.random.key(seed)
        x = 7.22e-05 + 1 * jax.random.normal(jax.random.fold_in(_gk, 1), (128, 128, 512), jnp.float32)
        _a = jax.random.bernoulli(jax.random.fold_in(_gk, 2), 0.125, (128, 128, 128))
        _a = jnp.logical_or(_a, jnp.swapaxes(_a, -1, -2))
        _a = jnp.logical_or(_a, jnp.eye(128, dtype=bool))
        _af = _a.astype(jnp.float32)
        _af = _af * jax.random.uniform(jax.random.fold_in(_gk, 3), (128, 128, 128), jnp.float32, 0.05, 4.42607)
        adj = _af
        return (x, adj)
    x, adj = _rec_inputs()

    def _L0_gnn_setup():
        import jax, jax.numpy as jnp
        import numpy as np
        NUM_HEADS = 16
        key = jax.random.key(seed)
        ks = jax.random.split(key, 7)
        B, N, D = (16, 256, 512)
        return {'x': jax.random.normal(ks[0], (B, N, D), dtype=jnp.float32), 'spatial_encoding': jax.random.normal(ks[1], (B, N, N), dtype=jnp.float32), 'edge_encoding': jax.random.normal(ks[2], (B, N, N), dtype=jnp.float32), 'Wq': jax.random.normal(ks[3], (D, D), dtype=jnp.float32) * D ** (-0.5), 'Wk': jax.random.normal(ks[4], (D, D), dtype=jnp.float32) * D ** (-0.5), 'Wv': jax.random.normal(ks[5], (D, D), dtype=jnp.float32) * D ** (-0.5), 'Wo': jax.random.normal(ks[6], (D, D), dtype=jnp.float32) * D ** (-0.5)}
    _L0_gnn_all = _L0_gnn_setup()
    _L0_gnn_in = {k: v for k, v in _L0_gnn_all.items() if k in ('Wq', 'Wk', 'Wv', 'Wo')}
    del _L0_gnn_all

    def _L1_gnn_setup():
        import jax, jax.numpy as jnp
        import numpy as np
        B, N, H, E = (64, 256, 512, 4)
        BN_EPS = 1e-05
        key = jax.random.key(seed)
        ks = jax.random.split(key, 6)
        x = jax.random.normal(ks[0], (B, N, H), dtype=jnp.float32)
        adj = jax.random.uniform(ks[1], (B, N, N), dtype=jnp.float32)
        stdv = 1.0 / np.sqrt(H)
        expert_w = jax.random.uniform(ks[2], (E, H, H), minval=-stdv, maxval=stdv, dtype=jnp.float32)
        r_std = 1.0 / np.sqrt(H)
        router_w = jax.random.uniform(ks[3], (H, E), minval=-r_std, maxval=r_std, dtype=jnp.float32)
        router_b = jax.random.uniform(ks[4], (E,), minval=-r_std, maxval=r_std, dtype=jnp.float32)
        bn_gamma = jnp.ones((E, H), dtype=jnp.float32)
        bn_beta = jnp.zeros((E, H), dtype=jnp.float32)
        return {'x': x, 'adj': adj, 'router_w': router_w, 'router_b': router_b, 'expert_w': expert_w, 'bn_gamma': bn_gamma, 'bn_beta': bn_beta}
    _L1_gnn_all = _L1_gnn_setup()
    _L1_gnn_in = {k: v for k, v in _L1_gnn_all.items() if k in ('router_w', 'router_b', 'expert_w', 'bn_gamma', 'bn_beta')}
    del _L1_gnn_all
    return {'x': x, 'adj': adj, 'L0_gnn_Wq': _L0_gnn_in['Wq'], 'L0_gnn_Wk': _L0_gnn_in['Wk'], 'L0_gnn_Wv': _L0_gnn_in['Wv'], 'L0_gnn_Wo': _L0_gnn_in['Wo'], 'L1_gnn_router_w': _L1_gnn_in['router_w'], 'L1_gnn_router_b': _L1_gnn_in['router_b'], 'L1_gnn_expert_w': _L1_gnn_in['expert_w'], 'L1_gnn_bn_gamma': _L1_gnn_in['bn_gamma'], 'L1_gnn_bn_beta': _L1_gnn_in['bn_beta']}

def reference(x, adj, L0_gnn_Wq, L0_gnn_Wk, L0_gnn_Wv, L0_gnn_Wo, L1_gnn_router_w, L1_gnn_router_b, L1_gnn_expert_w, L1_gnn_bn_gamma, L1_gnn_bn_beta):
    import jax
    import jax.numpy as jnp

    def _L0_gnn_ref(x, spatial_encoding, edge_encoding, Wq, Wk, Wv, Wo):
        import jax, jax.numpy as jnp
        import numpy as np
        NUM_HEADS = 16
        B, N, D = x.shape
        H = NUM_HEADS
        hd = D // H
        scale = D ** (-0.5)

        def split_heads(t):
            return t.reshape(B, N, H, hd).transpose(0, 2, 1, 3)
        q = split_heads(x @ Wq.T)
        k = split_heads(x @ Wk.T)
        v = split_heads(x @ Wv.T)
        bias = (spatial_encoding + edge_encoding)[:, None]
        a = jnp.einsum('bhnd,bhmd->bhnm', q, k) * scale + bias
        row_nonzero = jnp.any(a != 0, axis=-1, keepdims=True)
        a = jnp.where(row_nonzero, a, -jnp.inf)
        p = jax.nn.softmax(a, axis=-1)
        p = jnp.where(jnp.isnan(p), 0.0, p)
        o = jnp.einsum('bhnm,bhmd->bhnd', p, v)
        o = o.transpose(0, 2, 1, 3).reshape(B, N, D)
        return o @ Wo.T

    def _L1_gnn_ref(x, adj, router_w, router_b, expert_w, bn_gamma, bn_beta):
        import jax, jax.numpy as jnp
        import numpy as np
        B, N, H, E = (64, 256, 512, 4)
        BN_EPS = 1e-05
        scores = x.mean(axis=1) @ router_w + router_b
        top1 = jnp.argmax(scores, axis=-1)
        n_exp = expert_w.shape[0]
        W = expert_w[top1]
        support = jnp.einsum('bnh,bhk->bnk', x, W)
        out = jnp.einsum('bnm,bmk->bnk', adj, support)
        s = jax.ops.segment_sum(out.sum(axis=1), top1, num_segments=n_exp)
        ss = jax.ops.segment_sum((out * out).sum(axis=1), top1, num_segments=n_exp)
        cnt = jax.ops.segment_sum(jnp.ones_like(top1, dtype=out.dtype), top1, num_segments=n_exp) * out.shape[1]
        cnt = jnp.maximum(cnt, 1.0)[:, None]
        mean = s / cnt
        var = ss / cnt - mean * mean
        m = mean[top1][:, None, :]
        inv = jax.lax.rsqrt(var[top1][:, None, :] + BN_EPS)
        y = (out - m) * inv * bn_gamma[top1][:, None, :] + bn_beta[top1][:, None, :]
        return jax.nn.relu(y)
    x = _layernorm(x + _L0_gnn_ref(x, adj, adj, L0_gnn_Wq, L0_gnn_Wk, L0_gnn_Wv, L0_gnn_Wo), axis=-1)
    x = _layernorm(x + _L1_gnn_ref(x, adj, L1_gnn_router_w, L1_gnn_router_b, L1_gnn_expert_w, L1_gnn_bn_gamma, L1_gnn_bn_beta), axis=-1)
    return x

_drawn_inputs = setup_inputs


def setup_inputs(seed=0):
    import zlib

    import numpy as np

    out = dict(_drawn_inputs(seed))
    spreads = {'L1_gnn_bn_gamma': (1.0, 0.2), 'L1_gnn_bn_beta': (0.0, 0.1)}
    factors = {}
    for name, (base, spread) in spreads.items():
        noise = np.random.default_rng([zlib.crc32(name.encode()), seed]).standard_normal(out[name].shape)
        drawn = base * np.exp(spread * noise) if base else spread * noise
        out[name] = jnp.asarray(drawn.astype(out[name].dtype))
    for name, factor in factors.items():
        out[name] = (out[name] * factor).astype(out[name].dtype)
    return out
```

```python
from contextlib import ExitStack

import concourse.bass as bass
from concourse import mybir

F32 = mybir.dt.float32
F32R = mybir.dt.float32r
U32 = mybir.dt.uint32
ALU = mybir.AluOpType
ACT = mybir.ActivationFunctionType
AX_X = mybir.AxisListType.X

P = 128
HEADS = 16
EPS = 1e-5
BIG = 3.0e38
UNROLL = 4
GROUP = 2


def passes(hi_a, lo_a, hi_b, lo_b):
    return ((hi_a, hi_b), (hi_a, lo_b), (lo_a, hi_b))


def attention_phase(nc, io, W_hi, W_lo, mean_t, ident, ones, x1_dram, B, D):
    C = D // P
    HD = D // HEADS
    HC = P // HD
    SCALE = float(D) ** -0.5
    NG = B // GROUP
    GN = GROUP * P
    UNITS = 2 * C // GROUP
    AHEAD = 12
    Q, K, V, O = range(4)

    with ExitStack() as ctx:
        def sb(name, shape, dt=F32):
            return ctx.enter_context(nc.sbuf_tensor(name, shape, dt))

        def sem(name):
            return ctx.enter_context(nc.semaphore(name))

        w_stage = sb("w_stage", [P, 2, C, D])
        xt_stage = sb("xt_stage", [P, 2, C, GN])
        xt_hi = sb("xt_hi", [P, 2, C, GN], F32R)
        xt_lo = sb("xt_lo", [P, 2, C, GN], F32R)
        x_nat = sb("x_nat", [P, UNROLL, D])
        adj_nat = sb("adj_nat", [P, UNROLL, P])
        neg_bias = sb("neg_bias", [P, 2, P])
        qk = sb("qk", [P, 2, 2, C, GN])
        v_sb = sb("v_sb", [P, UNROLL, D])
        neg_s = sb("neg_s", [P, HEADS * P])
        probs = sb("probs", [P, HEADS * P])
        probs_t = sb("probs_t", [P, HEADS * P])
        o_hi = sb("o_hi", [P, C, P], F32R)
        o_lo = sb("o_lo", [P, C, P], F32R)
        res = sb("res", [P, 2, D])
        x1 = sb("x1", [P, UNROLL, D])
        neg_max = sb("neg_max", [P, HEADS])
        row_sum = sb("row_sum", [P, HEADS])
        abs_max = sb("abs_max", [P, HEADS])
        inv_sum = sb("inv_sum", [P, HEADS])
        row_scale = sb("row_scale", [P, HEADS])
        stats = sb("stats", [P, 2, 6])
        mean_var = sb("mean_var", [P, 2, 2])
        var_eps = sb("var_eps", [P, 2])
        rstd = sb("rstd", [P, 2])
        minus_half = sb("minus_half", [P, 1])

        bank = [ctx.enter_context(nc.psum_tensor(f"att_bank{i}", [P, D], F32)) for i in range(8)]
        BANK_A, BANK_B, BANK_O, BANK_WO = 4, 5, 6, 7

        w_in = [sem(f"w_in{i}") for i in range(4)]
        w_hi_done, w_lo_done = sem("w_hi_done"), sem("w_lo_done")
        xt_in = [sem(f"xt_in{i}") for i in range(2)]
        x_in = [sem(f"x_in{i}") for i in range(UNROLL)]
        adj_in = [sem(f"adj_in{i}") for i in range(UNROLL)]
        x1_out = [sem(f"x1_out{i}") for i in range(UNROLL)]
        xt_hi_done, xt_lo_done = sem("xt_hi_done"), sem("xt_lo_done")
        bias_done = sem("bias_done")
        qk_ps = sem("qk_ps")
        qk_done = [sem("qk_even_done"), sem("qk_odd_done")]
        v_ps, v_done = sem("v_ps"), sem("v_done")
        s_ps, min_done, abs_done = sem("s_ps"), sem("min_done"), sem("abs_done")
        exp_done, inv_done, scale_done = sem("exp_done"), sem("inv_done"), sem("scale_done")
        probs_done, pt_ps = sem("probs_done"), sem("pt_ps")
        pt_even, pt_odd = sem("pt_even"), sem("pt_odd")
        pv_ps, o_hi_done, o_lo_done, wo_ps = sem("pv_ps"), sem("o_hi_done"), sem("o_lo_done"), sem("wo_ps")
        res_done, stats_done, mv_done, ve_done = sem("res_done"), sem("stats_done"), sem("mv_done"), sem("ve_done")
        rstd_done, x1_done = sem("rstd_done"), sem("x1_done")
        sum_ps, sum_done = sem("sum_ps"), sem("sum_done")
        const_done, zero_done = sem("const_done"), sem("zero_done")

        LAST = B - UNROLL

        def for_steps(eng, body):
            with eng.Fori(0, LAST // UNROLL) as i:
                for s in range(UNROLL):
                    body(i * UNROLL + s, s, i, False)
            for s in range(UNROLL):
                body(LAST + s, s, LAST // UNROLL, True)

        def exists(step, last, ahead):
            return not last or step + ahead < B

        block = ctx.enter_context(nc.Block())

        @block.sync
        def _(sp):
            def load_xt(g, p):
                sp.dma_start(xt_stage[:, p], io["x_t"][g]).then_inc(xt_in[p], 16)

            def load_w(n):
                sp.dma_start(w_stage[:, n % 2], io["w"][n]).then_inc(w_in[n], 16)

            load_xt(0, 0)
            load_w(Q)
            load_w(K)
            load_xt(1, 1)
            sp.dma_start(adj_nat[:, 0], io["adj"][0]).then_inc(adj_in[0], 16)
            for n in (V, O):
                sp.wait_ge(w_lo_done, n - 1)
                load_w(n)
            for s in range(1, UNROLL):
                sp.dma_start(adj_nat[:, s], io["adj"][s]).then_inc(adj_in[s], 16)
            for s in range(UNROLL):
                sp.dma_start(x_nat[:, s], io["x"][s]).then_inc(x_in[s], 16)

            def body(t, s, i, last):
                if s % 2 == 0 and not last:
                    g = i * 2 + s // 2
                    sp.wait_ge(xt_lo_done, g + 1)
                    load_xt(g + 2, s // 2)
                if exists(t, last, UNROLL):
                    sp.wait_ge(bias_done, t + 1)
                    sp.dma_start(adj_nat[:, s], io["adj"][t + UNROLL]).then_inc(adj_in[s], 16)
                    sp.wait_ge(res_done, t + 2)
                    sp.dma_start(x_nat[:, s], io["x"][t + UNROLL]).then_inc(x_in[s], 16)
                sp.wait_ge(x1_done, t + 2)
                sp.dma_start(x1_dram[t], x1[:, s]).then_inc(x1_out[s], 16)

            for_steps(sp, body)
            for s in range(UNROLL):
                sp.wait_ge(x1_out[s], 16 * (B // UNROLL + 1))

        @block.tensor
        def _(pe):
            def qk_unit(n, c, which, par, b):
                dst = bank[b][:, 0:GN]
                todo = [(w, x, k) for w, x in passes(W_hi, W_lo, xt_hi, xt_lo) for k in range(C)]
                for m, (w, x, k) in enumerate(todo):
                    mm = pe.matmul(dst, w[:, which, k, c * P:(c + 1) * P], x[:, par, k, :],
                                   start=m == 0, stop=m == len(todo) - 1)
                mm.then_inc(qk_ps, 1)

            def v_parts(s, b):
                par, j = (s // 2) % 2, s % 2
                todo = [(x, w, k) for x, w in passes(xt_hi, xt_lo, W_hi, W_lo) for k in range(C)]
                for m, (x, w, k) in enumerate(todo):
                    mm = pe.matmul(bank[b][:, :], x[:, par, k, j * P:(j + 1) * P], w[:, V, k, :],
                                   start=m == 0, stop=m == len(todo) - 1)
                    if m == len(todo) - 1:
                        mm.then_inc(v_ps, 1)
                    yield

            def scores(s):
                par, j = (s // 2) % 2, s % 2
                for c in range(C):
                    for r in range(HC):
                        rows = slice(r * HD, (r + 1) * HD)
                        mm = pe.matmul(bank[r][:, c * P:(c + 1) * P],
                                       qk[rows, par, Q, c, j * P:(j + 1) * P],
                                       qk[rows, par, K, c, j * P:(j + 1) * P], start=True, stop=True)
                mm.then_inc(s_ps, 1)

            for n in range(8):
                if n == 0:
                    pe.wait_ge(xt_lo_done, 1)
                if n % C == 0:
                    pe.wait_ge(w_lo_done, n // C + 1)
                if n >= 2:
                    pe.wait_ge(qk_done[n % 2], n // 2)
                qk_unit(n, n % C, n // C, 0, BANK_B - n % 2)
            pe.wait_ge(w_lo_done, 3)
            for s in range(2):
                pe.wait_ge(qk_done[s], 4)
                for _ in v_parts(s, BANK_B - s):
                    pass
            pe.wait_ge(xt_lo_done, 2)
            for n in range(8, AHEAD):
                if n < 10:
                    pe.wait_ge(v_done, n - 7)
                else:
                    pe.wait_ge(qk_done[n % 2], n // 2)
                qk_unit(n, n % C, Q, 1, BANK_B - n % 2)
            scores(0)
            pe.wait_ge(w_lo_done, 4)
            pe.wait_ge(const_done, 3)

            def body(t, s, i, last):
                def transposes(c):
                    pe.wait_ge(probs_done, 4 * t + c + 1)
                    for r in range(HC):
                        h = c * HC + r
                        mm = pe.transpose(bank[c][:, r * P:(r + 1) * P], probs[:, h * P:(h + 1) * P],
                                          ident[:, :])
                    mm.then_inc(pt_ps, 1)

                def weighted_values(c):
                    pe.wait_ge(pt_odd if c % 2 else pt_even, 2 * t + c // 2 + 1)
                    for r in range(HC):
                        h = c * HC + r
                        mm = pe.matmul(bank[BANK_O][r * HD:(r + 1) * HD, c * P:(c + 1) * P],
                                       v_sb[:, s, h * HD:(h + 1) * HD], probs_t[:, h * P:(h + 1) * P],
                                       start=True, stop=True)
                    if c == C - 1:
                        mm.then_inc(pv_ps, 1)

                def some_values(n):
                    for _ in range(n):
                        next(values, None)

                if exists(t, last, 2):
                    pe.wait_ge(qk_done[1], AHEAD // 2 + 2 * t)
                    values = v_parts((s + 2) % UNROLL, BANK_A)
                else:
                    values = iter(())
                pe.wait_ge(v_done, t + 1)
                some_values(2)
                transposes(0)
                transposes(1)
                some_values(3)
                transposes(2)
                weighted_values(0)
                some_values(2)
                transposes(3)
                weighted_values(1)
                some_values(2)
                weighted_values(2)
                some_values(3)
                weighted_values(3)
                pe.wait_ge(x1_done, t + 1)
                pe.wait_ge(qk_done[0], min(AHEAD // 2 + 2 * t, C * NG) if last else AHEAD // 2 + 2 * t)
                for c in range(C):
                    mm = pe.matmul(bank[BANK_B][:, c:c + 1], x1[:, (s + 3) % UNROLL, c * P:(c + 1) * P],
                                   ones[:, 0:1], start=True, stop=True)
                mm.then_inc(sum_ps, 1)
                if exists(t, last, 1):
                    for done in qk_done:
                        pe.wait_ge(done, 2 * (t + 1 - (s + 1) % 2) + 4)
                    pe.wait_ge(pt_even, 2 * t + 2)
                    pe.wait_ge(pt_odd, 2 * t + 2)
                    scores((s + 1) % UNROLL)
                pe.wait_ge(o_lo_done, t + 1)
                pe.wait_ge(res_done, t + 1)
                todo = [(a, w, k) for a, w in passes(o_hi, o_lo, W_hi, W_lo) for k in range(C)]
                for m, (a, w, k) in enumerate(todo):
                    mm = pe.matmul(bank[BANK_WO][:, :], a[:, k, :], w[:, O, k, :],
                                   start=m == 0, stop=m == len(todo) - 1)
                mm.then_inc(wo_ps, 1)
                if exists(t, last, 3):
                    ahead = s + 3
                    if s % 2:
                        pe.wait_ge(xt_lo_done, i * 2 + ahead // 2 + 1)
                    for k in range(UNITS):
                        if k == 0:
                            pe.wait_ge(sum_done, t + 1)
                        elif k == 1:
                            pe.wait_ge(v_done, t + 3)
                        else:
                            pe.wait_ge(qk_done[k % 2], AHEAD // 2 + 2 * t + 1)
                        qk_unit(AHEAD + 4 * t + k, k, ahead % 2, (ahead // 2) % 2, BANK_B - k % 2)

            for_steps(pe, body)
            pe.wait_ge(x1_done, B + 1)
            pe.wait_ge(sum_done, B)
            for c in range(C):
                mm = pe.matmul(bank[BANK_B][:, c:c + 1], x1[:, UNROLL - 1, c * P:(c + 1) * P],
                               ones[:, 0:1], start=True, stop=True)
            mm.then_inc(sum_ps, 1)

        @block.scalar
        def _(act):
            def cut_w(n):
                act.wait_ge(w_in[n], 16)
                nc.scalar.activation(W_hi[:, n], w_stage[:, n % 2], ACT.Copy).then_inc(w_hi_done, 1)

            def copy_qk(n, c, which, par):
                act.wait_ge(qk_ps, n + 1)
                nc.scalar.activation(qk[:, par, which, c, :], bank[BANK_B][:, 0:GN], ACT.Copy,
                                     scale=-SCALE if which == Q else 1.0).then_inc(qk_done[0], 1)

            def exps(t, heads):
                for h in heads:
                    act.wait_ge(min_done, HEADS * t + h + 1)
                    nc.scalar.activation(probs[:, h * P:(h + 1) * P], neg_s[:, h * P:(h + 1) * P],
                                         ACT.Exp, bias=neg_max[:, h:h + 1], scale=-1.0,
                                         accum_out=row_sum[:, h:h + 1]).then_inc(exp_done, 1)

            def copy_v(t, s, b):
                act.wait_ge(v_ps, t + 1)
                nc.scalar.activation(v_sb[:, s, :], bank[b][:, :], ACT.Copy).then_inc(v_done, 1)

            cut_w(Q)
            cut_w(K)
            for n in range(8):
                if n == C:
                    act.wait_ge(w_lo_done, 1)
                    cut_w(V)
                if n % 2 == 0:
                    copy_qk(n, n % C, n // C, 0)
            cut_w(O)
            for s in range(2):
                copy_v(s, s, BANK_B - s)
            for n in range(8, AHEAD, 2):
                copy_qk(n, n % C, Q, 1)
            exps(0, range(HEADS))

            def body(t, s, i, last):
                for c in (1, 3):
                    act.wait_ge(pt_ps, 4 * t + c + 1)
                    nc.scalar.activation(probs_t[:, c * D:(c + 1) * D], bank[c][:, :],
                                         ACT.Copy).then_inc(pt_odd, 1)
                if exists(t, last, 2):
                    copy_v(t + 2, (s + 2) % UNROLL, BANK_A)
                act.wait_ge(pv_ps, t + 1)
                nc.scalar.activation(o_hi[:, :, :], bank[BANK_O][:, :].rearrange("p (c n) -> p c n", c=C),
                                     ACT.Copy).then_inc(o_hi_done, 1)
                ahead = s + 3
                for k in range(UNITS):
                    if exists(t, last, 1):
                        exps(t + 1, range(4 * k, 4 * k + 4) if k else range(0, 4))
                    if exists(t, last, 3) and k % 2 == 0:
                        copy_qk(AHEAD + 4 * t + k, k, ahead % 2, (ahead // 2) % 2)

            for_steps(act, body)

        @block.vector
        def _(dve):
            def cut_w(n):
                dve.wait_ge(w_hi_done, n + 1)
                nc.vector.tensor_tensor(W_lo[:, n], w_stage[:, n % 2], W_hi[:, n].bitcast(F32),
                                        ALU.subtract).then_inc(w_lo_done, 1)

            def cut_xt(g, p):
                dve.wait_ge(xt_in[p], 16)
                nc.vector.tensor_copy(xt_hi[:, p], xt_stage[:, p]).then_inc(xt_hi_done, 1)

            def copy_qk(n, c, which, par):
                dve.wait_ge(qk_ps, n + 1)
                nc.vector.tensor_scalar(qk[:, par, which, c, :], bank[BANK_A][:, 0:GN],
                                        -SCALE if which == Q else 1.0, None, ALU.mult).then_inc(qk_done[1], 1)

            def bias(t, s):
                dve.wait_ge(adj_in[s], (t - s) * 4 + 16)
                nc.vector.tensor_scalar(neg_bias[:, s % 2], adj_nat[:, s], -2.0, None,
                                        ALU.mult).then_inc(bias_done, 1)

            def minima(t, s):
                for h in range(HEADS):
                    c, r = h // HC, h % HC
                    nc.vector.tensor_tensor_reduce(neg_s[:, h * P:(h + 1) * P],
                                                   bank[r][:, c * P:(c + 1) * P], neg_bias[:, s % 2],
                                                   1.0, BIG, ALU.add, ALU.min,
                                                   neg_max[:, h:h + 1]).then_inc(min_done, 1)

            def largest(t, c):
                dve.wait_ge(min_done, HEADS * t + HC * (c + 1))
                heads = slice(c * HC, (c + 1) * HC)
                nc.vector.tensor_reduce(abs_max[:, heads],
                                        neg_s[:, c * D:(c + 1) * D].rearrange("p (h m) -> p h m", h=HC),
                                        AX_X, ALU.max, apply_absolute_value=True).then_inc(abs_done, 1)

            def inverse(t, c):
                heads = slice(c * HC, (c + 1) * HC)
                dve.wait_ge(exp_done, HEADS * t + HC * (c + 1))
                nc.vector.reciprocal(inv_sum[:, heads], row_sum[:, heads]).then_inc(inv_done, 1)

            def scales(t, c):
                heads = slice(c * HC, (c + 1) * HC)
                dve.wait_ge(inv_done, C * t + c + 1)
                dve.wait_ge(abs_done, C * t + c + 1)
                nc.vector.scalar_tensor_tensor(out=row_scale[:, heads], in0=abs_max[:, heads], scalar=0.0,
                                               in1=inv_sum[:, heads], op0=ALU.is_gt,
                                               op1=ALU.mult).then_inc(scale_done, 1)

            nc.vector.memset(x1[:, UNROLL - 1], 0.0).then_inc(zero_done, 1)
            dve.sem_inc(res_done, 1)
            dve.wait_ge(zero_done, 1)
            dve.sem_inc(x1_done, 1)
            cut_xt(0, 0)
            cut_w(Q)
            cut_w(K)
            bias(0, 0)
            cut_xt(1, 1)
            for n in range(8):
                if n == C:
                    cut_w(V)
                if n % 2:
                    copy_qk(n, n % C, n // C, 0)
            cut_w(O)
            for n in range(9, AHEAD, 2):
                copy_qk(n, n % C, Q, 1)
            dve.wait_ge(s_ps, 1)
            dve.wait_ge(bias_done, 1)
            minima(0, 0)
            for c in range(C):
                largest(0, c)
            for c in range(C):
                inverse(0, c)
                scales(0, c)

            def body(t, s, i, last):
                more = exists(t, last, 1)
                for c in (0, 2):
                    dve.wait_ge(pt_ps, 4 * t + c + 1)
                    nc.vector.tensor_copy(probs_t[:, c * D:(c + 1) * D], bank[c][:, :]).then_inc(pt_even, 1)
                    if c == 0 and more:
                        bias(t + 1, (s + 1) % UNROLL)
                    if c == 0 and s % 2 and not last:
                        dve.wait_ge(v_ps, t + 1)
                        dve.wait_ge(xt_in[s // 2], i * 16 + 32)
                        nc.vector.tensor_copy(xt_hi[:, s // 2], xt_stage[:, s // 2]).then_inc(xt_hi_done, 1)
                dve.wait_ge(o_hi_done, t + 1)
                nc.vector.tensor_tensor(o_lo[:, :, :], bank[BANK_O][:, :].rearrange("p (c n) -> p c n", c=C),
                                        o_hi[:, :, :].bitcast(F32), ALU.subtract).then_inc(o_lo_done, 1)
                if more:
                    dve.wait_ge(s_ps, t + 2)
                    dve.wait_ge(bias_done, t + 2)
                dve.wait_ge(sum_ps, t + 1)
                nc.vector.tensor_copy(mean_t[:, :, bass.ds(t, 1)],
                                      bank[BANK_B][:, 0:C].unsqueeze(2)).then_inc(sum_done, 1)
                if more:
                    minima(t + 1, s + 1)
                dve.wait_ge(wo_ps, t + 1)
                dve.wait_ge(x_in[s], i * 16 + 16)
                nc.vector.tensor_tensor(res[:, s % 2], bank[BANK_WO][:, :], x_nat[:, s],
                                        ALU.add).then_inc(res_done, 1)

                ahead = s + 3

                def copy_odd(k):
                    if exists(t, last, 3):
                        copy_qk(AHEAD + 4 * t + k, k, ahead % 2, (ahead // 2) % 2)

                if more:
                    largest(t + 1, 0)
                    inverse(t + 1, 0)
                dve.wait_ge(res_done, t + 2)
                nc.vector.bn_stats(stats[:, s % 2], res[:, s % 2]).then_inc(stats_done, 1)
                if more:
                    scales(t + 1, 0)
                    largest(t + 1, 1)
                dve.wait_ge(stats_done, t + 1)
                copy_odd(1)
                nc.vector.bn_aggr(mean_var[:, s % 2], stats[:, s % 2]).then_inc(mv_done, 1)
                if more:
                    inverse(t + 1, 1)
                    largest(t + 1, 2)
                    scales(t + 1, 1)
                dve.wait_ge(mv_done, t + 1)
                nc.vector.tensor_scalar(var_eps[:, s % 2:s % 2 + 1], mean_var[:, s % 2, 1:2], EPS, None,
                                        ALU.add).then_inc(ve_done, 1)
                if more:
                    inverse(t + 1, 2)
                    largest(t + 1, 3)
                    scales(t + 1, 2)
                copy_odd(3)
                dve.wait_ge(rstd_done, t + 1)
                dve.wait_ge(x1_out[s], i * 16 + 16)
                dve.wait_ge(sum_ps, t + 1)
                nc.vector.tensor_scalar(x1[:, s], res[:, s % 2], mean_var[:, s % 2, 0:1],
                                        rstd[:, s % 2:s % 2 + 1], ALU.subtract,
                                        ALU.mult).then_inc(x1_done, 1)
                if more:
                    inverse(t + 1, 3)
                    scales(t + 1, 3)

            for_steps(dve, body)
            dve.wait_ge(sum_ps, B + 1)
            nc.vector.tensor_copy(mean_t[:, :, B:B + 1], bank[BANK_B][:, 0:C].unsqueeze(2)).then_inc(sum_done, 1)

        @block.gpsimd
        def _(pool):
            for s in range(UNROLL):
                pool.sem_inc(x1_out[s], 16)
            nc.gpsimd.memset(minus_half[:, :], -0.5).then_inc(const_done, 1)
            nc.gpsimd.memset(ident[:, :], 0.0).then_inc(const_done, 1)
            nc.gpsimd.memset(ones[:, :], 1.0).then_inc(const_done, 1)
            pool.wait_ge(const_done, 3)
            nc.gpsimd.affine_select(out=ident[:, :], in_=ident[:, :], compare_op=ALU.not_equal, fill=1.0,
                                    base=0, pattern=[[-1, P]], channel_multiplier=1).then_inc(const_done, 1)

            def xt_low(g, p):
                pool.wait_ge(xt_hi_done, g + 1)
                nc.gpsimd.tensor_tensor(xt_lo[:, p], xt_stage[:, p], xt_hi[:, p].bitcast(F32),
                                        ALU.subtract).then_inc(xt_lo_done, 1)

            def normalise(t, c):
                pool.wait_ge(scale_done, C * t + c + 1)
                part = probs[:, c * D:(c + 1) * D].rearrange("p (h m) -> p h m", h=HC)
                by = row_scale[:, c * HC:(c + 1) * HC].unsqueeze(2).to_broadcast([P, HC, P])
                nc.gpsimd.tensor_tensor(part, part, by, ALU.mult).then_inc(probs_done, 1)

            xt_low(0, 0)
            xt_low(1, 1)
            for c in range(C):
                normalise(0, c)

            def body(t, s, i, last):
                if s % 2 and not last:
                    xt_low(i * 2 + s // 2 + 2, s // 2)
                if exists(t, last, 1):
                    normalise(t + 1, 0)
                    normalise(t + 1, 1)
                pool.wait_ge(ve_done, t + 1)
                nc.gpsimd.tensor_tensor(rstd[:, s % 2:s % 2 + 1], var_eps[:, s % 2:s % 2 + 1],
                                        minus_half[:, :], ALU.pow).then_inc(rstd_done, 1)
                if exists(t, last, 1):
                    normalise(t + 1, 2)
                    normalise(t + 1, 3)

            for_steps(pool, body)


def router_phase(nc, io, mean_t, ident, ones, expert_row, count_col, B, D, E):
    C = D // P
    with ExitStack() as ctx:
        def sb(name, shape, dt=F32):
            return ctx.enter_context(nc.sbuf_tensor(name, shape, dt))

        def sem(name):
            return ctx.enter_context(nc.semaphore(name))

        router_w = sb("router_w", [P, C, E])
        router_b = sb("router_b", [P, E])
        scores = sb("scores", [P, 8])
        best = sb("best", [P, 8])
        best_at = sb("best_at", [P, 8], U32)
        expert = sb("expert", [P, 1])
        numbers = sb("numbers", [P, E])
        one_hot = sb("one_hot", [P, E])
        ps_scores = ctx.enter_context(nc.psum_tensor("ps_scores", [P, E], F32))
        ps_count = ctx.enter_context(nc.psum_tensor("ps_count", [P, E], F32))
        ps_row = ctx.enter_context(nc.psum_tensor("ps_row", [1, P], F32))
        w_in, scores_ps, step = sem("rw_in"), sem("scores_ps"), sem("router_step")
        filled, expert_done, count_ps, row_ps = sem("filled"), sem("expert_done"), sem("count_ps"), sem("row_ps")

        block = ctx.enter_context(nc.Block())

        @block.sync
        def _(sp):
            sp.dma_start(router_w[:, :, :], io["router_w"].rearrange("(c p) e -> p c e", p=P)).then_inc(w_in, 16)
            sp.dma_start(router_b[:, :], io["router_b"].unsqueeze(0).to_broadcast([P, E])).then_inc(w_in, 16)

        @block.gpsimd
        def _(pool):
            nc.gpsimd.memset(scores[:, :], -BIG).then_inc(filled, 1)
            for e in range(E):
                nc.gpsimd.memset(numbers[:, e:e + 1], float(e)).then_inc(filled, 1)

        @block.tensor
        def _(pe):
            pe.wait_ge(w_in, 32)
            for c in range(C):
                mm = pe.matmul(ps_scores[:, :], mean_t[:, c, 1:B + 1], router_w[:, c, :],
                               start=c == 0, stop=c == C - 1)
            mm.then_inc(scores_ps, 1)
            pe.wait_ge(expert_done, 1)
            pe.transpose(ps_row[:, :], expert[:, :], ident[:, :]).then_inc(row_ps, 1)
            pe.wait_ge(expert_done, 2)
            pe.matmul(ps_count[:, :], ones[:, :], one_hot[:, :], start=True, stop=True).then_inc(count_ps, 1)

        @block.vector
        def _(dve):
            dve.wait_ge(scores_ps, 1)
            dve.wait_ge(filled, 1 + E)
            nc.vector.scalar_tensor_tensor(out=scores[:, 0:E], in0=ps_scores[:, :], scalar=1.0 / P,
                                           in1=router_b[:, :], op0=ALU.mult, op1=ALU.add).then_inc(step, 1)
            dve.wait_ge(step, 1)
            nc.vector.max(best[:, :], scores[:, :]).then_inc(step, 1)
            dve.wait_ge(step, 2)
            nc.vector.max_index(best_at[:, :], best[:, :], scores[:, :]).then_inc(step, 1)
            dve.wait_ge(step, 3)
            nc.vector.tensor_copy(expert[:, :], best_at[:, 0:1]).then_inc(expert_done, 1)
            dve.wait_ge(expert_done, 1)
            nc.vector.tensor_scalar(one_hot[:, :], numbers[:, :], expert[:, 0:1], None,
                                    ALU.is_equal).then_inc(expert_done, 1)
            dve.wait_ge(row_ps, 1)
            nc.vector.tensor_copy(expert_row[:, :], ps_row[:, :])
            dve.wait_ge(count_ps, 1)
            nc.vector.tensor_scalar(count_col[:, :], ps_count[:, :], float(P), 1.0, ALU.mult, ALU.max)


def expert_phase(nc, io, W_hi, W_lo, expert_row, out_sum, out_sq, x1_dram, y_dram, B, D, E):
    C = D // P
    LAST = B - UNROLL
    with ExitStack() as ctx:
        def sb(name, shape, dt=F32):
            return ctx.enter_context(nc.sbuf_tensor(name, shape, dt))

        def sem(name):
            return ctx.enter_context(nc.semaphore(name))

        e_stage = sb("e_stage", [P, 2, C, D])
        x1 = sb("g_x1", [P, UNROLL, D])
        adj_t = sb("adj_t", [P, UNROLL, P])
        y_hi, y_lo = sb("y_hi", [P, 2, D], F32R), sb("y_lo", [P, 2, D], F32R)
        out = sb("g_out", [P, UNROLL, D])
        sq = sb("g_sq", [P, 2, D])
        ps_y = [ctx.enter_context(nc.psum_tensor(f"ps_y{i}", [P, D], F32)) for i in range(2)]
        ps_o = [ctx.enter_context(nc.psum_tensor(f"ps_o{i}", [P, D], F32)) for i in range(2)]

        e_in = [sem(f"e_in{i}") for i in range(4)]
        e_hi_done, e_lo_done = sem("e_hi_done"), sem("e_lo_done")
        x1_in = [sem(f"g_x1_in{i}") for i in range(UNROLL)]
        adj_in = [sem(f"g_adj_in{i}") for i in range(UNROLL)]
        out_stored = [sem(f"out_stored{i}") for i in range(UNROLL)]
        y_ps, y_hi_done, y_lo_done = sem("y_ps"), sem("y_hi_done"), sem("y_lo_done")
        out_ps, out_done, sq_done = sem("out_ps"), sem("out_done"), sem("sq_done")
        zeroed, sum_done, sqsum_done = sem("zeroed"), sem("acc_sum_done"), sem("acc_sq_done")

        def for_steps(eng, body):
            with eng.Fori(0, LAST // UNROLL) as i:
                for s in range(UNROLL):
                    body(i * UNROLL + s, s, i, False)
            for s in range(UNROLL):
                body(LAST + s, s, LAST // UNROLL, True)

        def exists(step, last, ahead):
            return not last or step + ahead < B

        block = ctx.enter_context(nc.Block())

        @block.sync
        def _(sp):
            def load(t, s):
                sp.dma_start(x1[:, s], x1_dram[t]).then_inc(x1_in[s], 16)
                sp.dma_start(adj_t[:, s], io["adj_t"][t]).then_inc(adj_in[s], 16)

            for e in range(E):
                if e >= 2:
                    sp.wait_ge(e_lo_done, e - 1)
                sp.dma_start(e_stage[:, e % 2], io["expert_w"][e].rearrange("(c p) k -> p c k", p=P))\
                  .then_inc(e_in[e], 16)
                if e == 1:
                    for s in range(UNROLL):
                        load(s, s)

            def body(t, s, i, last):
                if exists(t, last, UNROLL):
                    sp.wait_ge(y_ps, t + 1)
                    load(t + UNROLL, s)
                sp.wait_ge(out_done, t + 3)
                sp.dma_start(y_dram[t], out[:, s]).then_inc(out_stored[s], 16)

            for_steps(sp, body)
            for s in range(UNROLL):
                sp.wait_ge(out_stored[s], 16 * (B // UNROLL + 1))

        @block.tensor
        def _(pe):
            def y_product(t, s):
                p = s % 2
                pe.wait_ge(x1_in[s], 4 * (t - s) + 16)
                pe.wait_ge(adj_in[s], 4 * (t - s) + 16)
                pe.wait_ge(y_lo_done, t + 1)
                for c in range(C):
                    mm = pe.matmul(ps_y[p][:, c * P:(c + 1) * P], x1[:, s, c * P:(c + 1) * P],
                                   adj_t[:, s, :], start=True, stop=True)
                mm.then_inc(y_ps, 1)

            def out_product(t, s):
                p = s % 2
                e = pe.value_load(expert_row[0:1, bass.ds(t, 1)], min_val=0, max_val=E - 1)
                pe.wait_ge(y_lo_done, t + 3)
                pe.wait_ge(out_done, t + 1)
                todo = [(a, w, k) for a, w in passes(y_hi, y_lo, W_hi, W_lo) for k in range(C)]
                for m, (a, w, k) in enumerate(todo):
                    mm = pe.matmul(ps_o[p][:, :], a[:, p, k * P:(k + 1) * P],
                                   w[:, bass.ds(e, 1), k, :].rearrange("p a n -> p (a n)"),
                                   start=m == 0, stop=m == len(todo) - 1)
                mm.then_inc(out_ps, 1)

            y_product(0, 0)
            pe.wait_ge(e_lo_done, E)

            def body(t, s, i, last):
                if exists(t, last, 1):
                    y_product(t + 1, (s + 1) % UNROLL)
                out_product(t, s)

            for_steps(pe, body)

        @block.scalar
        def _(act):
            def y_high(t, s):
                act.wait_ge(y_ps, t + 1)
                nc.scalar.activation(y_hi[:, s % 2], ps_y[s % 2][:, :], ACT.Copy).then_inc(y_hi_done, 1)

            for e in range(E):
                act.wait_ge(e_in[e], 16)
                nc.scalar.activation(W_hi[:, e], e_stage[:, e % 2], ACT.Copy).then_inc(e_hi_done, 1)
            y_high(0, 0)

            def body(t, s, i, last):
                if exists(t, last, 1):
                    y_high(t + 1, (s + 1) % UNROLL)
                act.wait_ge(out_done, t + 3)
                act.wait_ge(sqsum_done, t + 1)
                nc.scalar.activation(sq[:, s % 2], out[:, s], ACT.Square).then_inc(sq_done, 1)

            for_steps(act, body)

        @block.vector
        def _(dve):
            def y_low(t, s):
                dve.wait_ge(y_hi_done, t + 1)
                nc.vector.tensor_tensor(y_lo[:, s % 2], ps_y[s % 2][:, :], y_hi[:, s % 2].bitcast(F32),
                                        ALU.subtract).then_inc(y_lo_done, 1)

            dve.sem_inc(y_lo_done, 2)
            dve.sem_inc(out_done, 2)
            for e in range(E):
                dve.wait_ge(e_hi_done, e + 1)
                nc.vector.tensor_tensor(W_lo[:, e], e_stage[:, e % 2], W_hi[:, e].bitcast(F32),
                                        ALU.subtract).then_inc(e_lo_done, 1)
            y_low(0, 0)

            def body(t, s, i, last):
                if exists(t, last, 1):
                    y_low(t + 1, (s + 1) % UNROLL)
                dve.wait_ge(out_ps, t + 1)
                dve.wait_ge(out_stored[s], i * 16 + 16)
                dve.wait_ge(sum_done, t + 1)
                nc.vector.tensor_copy(out[:, s], ps_o[s % 2][:, :]).then_inc(out_done, 1)

            for_steps(dve, body)

        @block.gpsimd
        def _(pool):
            for s in range(UNROLL):
                pool.sem_inc(out_stored[s], 16)
            pool.sem_inc(sum_done, UNROLL)
            pool.sem_inc(sqsum_done, 2)
            nc.gpsimd.memset(out_sum[:, :, :], 0.0).then_inc(zeroed, 1)
            nc.gpsimd.memset(out_sq[:, :, :], 0.0).then_inc(zeroed, 1)
            pool.wait_ge(zeroed, 2)

            def body(t, s, i, last):
                e = pool.value_load(expert_row[0:1, bass.ds(t, 1)], min_val=0, max_val=E - 1)
                pool.wait_ge(out_done, t + 3)
                pool.wait_ge(sum_done, t + UNROLL)
                acc = out_sum[:, bass.ds(e, 1), :].rearrange("p a n -> p (a n)")
                nc.gpsimd.tensor_tensor(acc, acc, out[:, s], ALU.add).then_inc(sum_done, 1)
                pool.wait_ge(sq_done, t + 1)
                pool.wait_ge(sqsum_done, t + 2)
                acc = out_sq[:, bass.ds(e, 1), :].rearrange("p a n -> p (a n)")
                nc.gpsimd.tensor_tensor(acc, acc, sq[:, s % 2], ALU.add).then_inc(sqsum_done, 1)

            for_steps(pool, body)


def norm_phase(nc, io, ident, ones, expert_row, count_col, out_sum, out_sq, x1_dram, y_dram, out_dram, B, D, E):
    C = D // P
    N = E * C
    RING = 8
    LAST = B - UNROLL
    with ExitStack() as ctx:
        def sb(name, shape, dt=F32):
            return ctx.enter_context(nc.sbuf_tensor(name, shape, dt))

        def sem(name):
            return ctx.enter_context(nc.semaphore(name))

        gamma, beta = sb("gamma", [P, N]), sb("beta", [P, N])
        inv_count = sb("inv_count", [P, E])
        mean, msq, mean2 = sb("bn_mean", [P, N]), sb("bn_msq", [P, N]), sb("bn_mean2", [P, N])
        var_eps, inv = sb("bn_var_eps", [P, N]), sb("bn_inv", [P, N])
        half_n, half_u = sb("half_n", [P, N]), sb("half_u", [P, UNROLL])
        mul_col, m_mul, add_col = sb("mul_col", [P, N]), sb("m_mul", [P, N]), sb("add_col", [P, N])
        diag = sb("diag", [P, 2, N, P])
        mul_row, add_row = sb("mul_row", [P, E, D]), sb("add_row", [P, E, D])
        y = sb("n_y", [P, RING, D])
        x1 = sb("n_x1", [P, RING, D])
        scaled = sb("scaled", [P, 2, D])
        shifted = sb("shifted", [P, 2, D])
        z = sb("n_z", [P, RING, D])
        outs = sb("n_out", [P, UNROLL, D])
        stats = sb("n_stats", [P, UNROLL, 6])
        m_diff, m_sum, v_sum = sb("m_diff", [P, UNROLL]), sb("m_sum", [P, UNROLL]), sb("v_sum", [P, UNROLL])
        m_diff2, v_eps = sb("m_diff2", [P, UNROLL]), sb("v_eps", [P, UNROLL])
        ve, nm = sb("n_ve", [P, 2, UNROLL]), sb("n_nm", [P, 2, UNROLL])
        rstd, nb = sb("n_rstd", [P, 2, UNROLL]), sb("n_nb", [P, 2, UNROLL])
        ps_cols = ctx.enter_context(nc.psum_tensor("ps_cols", [P, 2, N], F32))
        ps_rows = [ctx.enter_context(nc.psum_tensor(f"ps_rows{i}", [P, D], F32)) for i in range(2)]

        gb_in, cols_ps, step, inv_done = sem("gb_in"), sem("cols_ps"), sem("bn_step"), sem("bn_inv_done")
        halves, diag_done, rows_ps, rows_done = sem("halves"), sem("diag_done"), sem("rows_ps"), sem("rows_done")
        y_in = [sem(f"n_y_in{i}") for i in range(RING)]
        x1_in = [sem(f"n_x1_in{i}") for i in range(RING)]
        stored = [sem(f"stored{i}") for i in range(UNROLL)]
        scaled_done, shifted_done, z_done = sem("scaled_done"), sem("shifted_done"), sem("z_done")
        stats_done, mv_done, ve_done = sem("n_stats_done"), sem("n_mv_done"), sem("n_ve_done")
        rstd_done, nb_done, out_done = sem("n_rstd_done"), sem("nb_done"), sem("n_out_done")

        ROUNDS = B // RING

        def for_steps(eng, body):
            with eng.Fori(0, ROUNDS - 1) as i:
                for s in range(RING):
                    body(i * RING + s, s, i, False)
            for s in range(RING):
                body((ROUNDS - 1) * RING + s, s, ROUNDS - 1, True)

        block = ctx.enter_context(nc.Block())

        @block.sync
        def _(sp):
            sp.dma_start(gamma[:, :], io["gamma"]).then_inc(gb_in, 16)
            sp.dma_start(beta[:, :], io["beta"]).then_inc(gb_in, 16)

            def load(t, s):
                sp.dma_start(y[:, s], y_dram[t]).then_inc(y_in[s], 16)
                sp.dma_start(x1[:, s], x1_dram[t]).then_inc(x1_in[s], 16)

            for s in range(RING):
                load(s, s)

            def body(t, s, i, last):
                if not last:
                    sp.wait_ge(z_done, t + 1)
                    load(t + RING, s)

            for_steps(sp, body)

        @block.tensor
        def _(pe):
            for w, acc in enumerate((out_sum, out_sq)):
                for e in range(E):
                    for c in range(C):
                        mm = pe.matmul(ps_cols[:, w, e * C + c:e * C + c + 1], acc[:, e, c * P:(c + 1) * P],
                                       ones[:, 0:1], start=True, stop=True)
            mm.then_inc(cols_ps, 1)
            for w in range(2):
                pe.wait_ge(diag_done, w + 1)
                for e in range(E):
                    n = w * E + e
                    if n >= 2:
                        pe.wait_ge(rows_done, n - 1)
                    for c in range(C):
                        mm = pe.matmul(ps_rows[n % 2][:, c * P:(c + 1) * P], ones[:, :],
                                       diag[:, w, e * C + c, :], start=True, stop=True)
                    mm.then_inc(rows_ps, 1)

        @block.vector
        def _(dve):
            count = [0]

            def chain(instruction):
                count[0] += 1
                instruction.then_inc(step, 1)
                dve.wait_ge(step, count[0])

            by_expert = "p (e c) -> p e c"
            over = inv_count[:, :].unsqueeze(2).to_broadcast([P, E, C])
            chain(nc.vector.reciprocal(inv_count[:, :], count_col[:, :]))
            dve.wait_ge(cols_ps, 1)
            chain(nc.vector.tensor_tensor(mean[:, :].rearrange(by_expert, e=E),
                                          ps_cols[:, 0, :].rearrange(by_expert, e=E), over, ALU.mult))
            chain(nc.vector.tensor_tensor(msq[:, :].rearrange(by_expert, e=E),
                                          ps_cols[:, 1, :].rearrange(by_expert, e=E), over, ALU.mult))
            chain(nc.vector.tensor_tensor(mean2[:, :], mean[:, :], mean[:, :], ALU.mult))
            chain(nc.vector.scalar_tensor_tensor(out=var_eps[:, :], in0=msq[:, :], scalar=EPS, in1=mean2[:, :],
                                                 op0=ALU.add, op1=ALU.subtract))
            dve.wait_ge(gb_in, 32)
            dve.wait_ge(inv_done, 1)
            chain(nc.vector.tensor_tensor(mul_col[:, :], inv[:, :], gamma[:, :], ALU.mult))
            chain(nc.vector.tensor_tensor(m_mul[:, :], mean[:, :], mul_col[:, :], ALU.mult))
            chain(nc.vector.tensor_tensor(add_col[:, :], beta[:, :], m_mul[:, :], ALU.subtract))
            for w, col in enumerate((mul_col, add_col)):
                for n in range(N):
                    ins = nc.vector.tensor_scalar(diag[:, w, n, :], ident[:, :], col[:, n:n + 1], None, ALU.mult)
                ins.then_inc(diag_done, 1)
            for w, row in enumerate((mul_row, add_row)):
                for e in range(E):
                    n = w * E + e
                    dve.wait_ge(rows_ps, n + 1)
                    nc.vector.tensor_copy(row[:, e, :], ps_rows[n % 2][:, :]).then_inc(rows_done, 1)
            dve.wait_ge(rows_done, 2 * E)

            def body(t, s, i, last):
                u = s // UNROLL
                e = dve.value_load(expert_row[0:1, bass.ds(t, 1)], min_val=0, max_val=E - 1)
                dve.wait_ge(scaled_done, t + 1)
                nc.vector.tensor_tensor(shifted[:, s % 2], scaled[:, s % 2],
                                        add_row[:, bass.ds(e, 1), :].rearrange("p a n -> p (a n)"),
                                        ALU.add).then_inc(shifted_done, 1)
                dve.wait_ge(shifted_done, t + 1)
                dve.wait_ge(x1_in[s], i * 16 + 16)
                dve.wait_ge(out_done, t + 1)
                nc.vector.scalar_tensor_tensor(out=z[:, s], in0=shifted[:, s % 2], scalar=0.0, in1=x1[:, s],
                                               op0=ALU.max, op1=ALU.add).then_inc(z_done, 1)
                dve.wait_ge(z_done, t + 1)
                nc.vector.bn_stats(stats[:, s % UNROLL], z[:, s]).then_inc(stats_done, 1)
                if s % UNROLL == UNROLL - 1:
                    r = i * 2 + u
                    dve.wait_ge(stats_done, t + 1)
                    nc.vector.tensor_tensor(m_diff[:, :], stats[:, :, 1], stats[:, :, 4],
                                            ALU.subtract).then_inc(mv_done, 1)
                    nc.vector.tensor_tensor(m_sum[:, :], stats[:, :, 1], stats[:, :, 4],
                                            ALU.add).then_inc(mv_done, 1)
                    nc.vector.tensor_tensor(v_sum[:, :], stats[:, :, 2], stats[:, :, 5],
                                            ALU.add).then_inc(mv_done, 1)
                    dve.wait_ge(mv_done, r * 5 + 3)
                    nc.vector.scalar_tensor_tensor(out=m_diff2[:, :], in0=m_diff[:, :], scalar=0.25,
                                                   in1=m_diff[:, :], op0=ALU.mult,
                                                   op1=ALU.mult).then_inc(mv_done, 1)
                    nc.vector.tensor_scalar(v_eps[:, :], v_sum[:, :], 1.0 / D, EPS, ALU.mult,
                                            ALU.add).then_inc(mv_done, 1)
                    nc.vector.tensor_scalar(nm[:, u, :], m_sum[:, :], -0.5, None, ALU.mult).then_inc(ve_done, 1)
                    dve.wait_ge(mv_done, r * 5 + 5)
                    nc.vector.tensor_tensor(ve[:, u, :], v_eps[:, :], m_diff2[:, :], ALU.add).then_inc(ve_done, 1)

            for_steps(dve, body)

        @block.gpsimd
        def _(pool):
            pool.sem_inc(out_done, RING)
            for s in range(UNROLL):
                pool.sem_inc(stored[s], 16)
            nc.gpsimd.memset(half_n[:, :], -0.5).then_inc(halves, 1)
            nc.gpsimd.memset(half_u[:, :], -0.5).then_inc(halves, 1)
            pool.wait_ge(halves, 2)
            pool.wait_ge(step, 5)
            nc.gpsimd.tensor_tensor(inv[:, :], var_eps[:, :], half_n[:, :], ALU.pow).then_inc(inv_done, 1)
            pool.wait_ge(rows_done, E)

            def body(t, s, i, last):
                e = pool.value_load(expert_row[0:1, bass.ds(t, 1)], min_val=0, max_val=E - 1)
                pool.wait_ge(y_in[s], i * 16 + 16)
                if s % UNROLL >= 2:
                    pool.wait_ge(shifted_done, t - 1)
                nc.gpsimd.tensor_tensor(scaled[:, s % 2], y[:, s],
                                        mul_row[:, bass.ds(e, 1), :].rearrange("p a n -> p (a n)"),
                                        ALU.mult).then_inc(scaled_done, 1)
                if s % UNROLL == UNROLL - 1:
                    u = s // UNROLL
                    r = i * 2 + u
                    pool.wait_ge(ve_done, r * 2 + 2)
                    nc.gpsimd.tensor_tensor(rstd[:, u, :], ve[:, u, :], half_u[:, :], ALU.pow).then_inc(rstd_done, 1)
                    pool.wait_ge(rstd_done, r + 1)
                    nc.gpsimd.tensor_tensor(nb[:, u, :], nm[:, u, :], rstd[:, u, :], ALU.mult).then_inc(nb_done, 1)

            for_steps(pool, body)

        @block.scalar
        def _(act):
            def body(t, s, i, last):
                u, k = s // UNROLL, s % UNROLL
                act.wait_ge(nb_done, i * 2 + u + 1)
                act.wait_ge(stored[k], (i * 2 + u) * 16 + 16)
                nc.scalar.activation(outs[:, k], z[:, s], ACT.Identity, bias=nb[:, u, k:k + 1],
                                     scale=rstd[:, u, k:k + 1]).then_inc(out_done, 1)
                act.wait_ge(out_done, t + RING + 1)
                act.dma_start(out_dram[t], outs[:, k]).then_inc(stored[k], 16)

            for_steps(act, body)
            for s in range(UNROLL):
                act.wait_ge(stored[s], 16 * (B // UNROLL + 1))


def build(nc, io, out_dram, B, D, E):
    C = D // P
    x1_dram = nc.dram_tensor("x1_scratch", [B, P, D], F32, kind="Internal").ap()
    y_dram = nc.dram_tensor("y_scratch", [B, P, D], F32, kind="Internal").ap()
    with ExitStack() as ctx:
        def sb(name, shape, dt=F32):
            return ctx.enter_context(nc.sbuf_tensor(name, shape, dt))

        mean_t = sb("mean_t", [P, C, B + 1])
        ident = sb("ident", [P, P])
        ones = sb("ones", [P, P])
        expert_row = sb("expert_row", [1, B], U32)
        count_col = sb("count_col", [P, E])
        def cut_weights(phase, inner):
            hi = inner.enter_context(nc.sbuf_tensor(f"{phase}_hi", [P, 4, C, D], F32R))
            lo = inner.enter_context(nc.sbuf_tensor(f"{phase}_lo", [P, 4, C, D], F32R))
            return hi, lo

        with ExitStack() as inner:
            W_hi, W_lo = cut_weights("att_w", inner)
            attention_phase(nc, io, W_hi, W_lo, mean_t, ident, ones, x1_dram, B, D)
        router_phase(nc, io, mean_t, ident, ones, expert_row, count_col, B, D, E)
        out_sum, out_sq = sb("out_sum", [P, E, D]), sb("out_sq", [P, E, D])
        with ExitStack() as inner:
            W_hi, W_lo = cut_weights("exp_w", inner)
            expert_phase(nc, io, W_hi, W_lo, expert_row, out_sum, out_sq, x1_dram, y_dram, B, D, E)
        norm_phase(nc, io, ident, ones, expert_row, count_col, out_sum, out_sq, x1_dram, y_dram, out_dram,
                   B, D, E)


def kernel(x, adj, L0_gnn_Wq, L0_gnn_Wk, L0_gnn_Wv, L0_gnn_Wo, L1_gnn_router_w, L1_gnn_router_b,
           L1_gnn_expert_w, L1_gnn_bn_gamma, L1_gnn_bn_beta):
    import numpy as np
    import concourse.bacc as bacc
    from concourse.bass_utils import run_bass_kernel_spmd

    x, adj = np.asarray(x), np.asarray(adj)
    B, n, D = x.shape
    E = L1_gnn_expert_w.shape[0]
    C = D // P

    def features_first(w):
        return np.asarray(w).T.reshape(C, P, D).transpose(1, 0, 2)

    arrays = {
        "x": x,
        "x_t": x.reshape(B // GROUP, GROUP, n, C, P).transpose(0, 4, 3, 1, 2).reshape(B // GROUP, P, C, GROUP * n),
        "adj": adj,
        "adj_t": adj.transpose(0, 2, 1),
        "w": np.stack([features_first(w) for w in (L0_gnn_Wq, L0_gnn_Wk, L0_gnn_Wv, L0_gnn_Wo)]),
        "router_w": np.asarray(L1_gnn_router_w),
        "router_b": np.asarray(L1_gnn_router_b),
        "expert_w": np.asarray(L1_gnn_expert_w),
        "gamma": np.asarray(L1_gnn_bn_gamma).reshape(E * C, P).T,
        "beta": np.asarray(L1_gnn_bn_beta).reshape(E * C, P).T,
    }
    nc = bacc.Bacc("TRN2", target_bir_lowering=False, num_devices=1)
    io, maps = {}, {}
    for name, a in arrays.items():
        a = np.ascontiguousarray(a)
        maps[f"in_{name}"] = a
        io[name] = nc.dram_tensor(f"in_{name}", a.shape, mybir.dt.from_np(a.dtype), kind="ExternalInput").ap()
    out = nc.dram_tensor("out_x", [B, n, D], F32, kind="ExternalOutput").ap()
    build(nc, io, out, B, D, E)
    r = run_bass_kernel_spmd(nc, [maps], core_ids=[0])
    return r.results[0]["out_x"]
```

```python
from contextlib import ExitStack

import concourse.bass as bass
from concourse import mybir

F32 = mybir.dt.float32
F32R = mybir.dt.float32r
U32 = mybir.dt.uint32
ALU = mybir.AluOpType
ACT = mybir.ActivationFunctionType
AX_X = mybir.AxisListType.X

P = 128
HEADS = 16
EPS = 1e-5
BIG = 3.0e38
UNROLL = 4
GROUP = 2


def passes(hi_a, lo_a, hi_b, lo_b):
    return ((hi_a, hi_b), (hi_a, lo_b), (lo_a, hi_b))


def attention_phase(nc, io, W_hi, W_lo, ident, x1_dram, B, D):
    C = D // P
    HD = D // HEADS
    HC = P // HD
    SCALE = float(D) ** -0.5
    NG = B // GROUP
    GN = GROUP * P
    UNITS = 2 * C // GROUP
    AHEAD = 12
    Q, K, V, O = range(4)

    with ExitStack() as ctx:
        def sb(name, shape, dt=F32):
            return ctx.enter_context(nc.sbuf_tensor(name, shape, dt))

        def sem(name):
            return ctx.enter_context(nc.semaphore(name))

        w_stage = sb("w_stage", [P, 2, C, D])
        xt_stage = sb("xt_stage", [P, 2, C, GN])
        xt_hi = sb("xt_hi", [P, 2, C, GN], F32R)
        xt_lo = sb("xt_lo", [P, 2, C, GN], F32R)
        x_nat = sb("x_nat", [P, UNROLL, D])
        adj_nat = sb("adj_nat", [P, UNROLL, P])
        neg_bias = sb("neg_bias", [P, 2, P])
        qk = sb("qk", [P, 2, 2, C, GN])
        v_sb = sb("v_sb", [P, UNROLL, D])
        neg_s = sb("neg_s", [P, HEADS * P])
        probs = sb("probs", [P, HEADS * P])
        probs_t = sb("probs_t", [P, HEADS * P])
        o_hi = sb("o_hi", [P, C, P], F32R)
        o_lo = sb("o_lo", [P, C, P], F32R)
        res = sb("res", [P, 2, D])
        x1 = sb("x1", [P, UNROLL, D])
        neg_max = sb("neg_max", [P, HEADS])
        row_sum = sb("row_sum", [P, HEADS])
        abs_max = sb("abs_max", [P, HEADS])
        inv_sum = sb("inv_sum", [P, HEADS])
        row_scale = sb("row_scale", [P, HEADS])
        stats = sb("stats", [P, 2, 6])
        mean_var = sb("mean_var", [P, 2, 2])
        var_eps = sb("var_eps", [P, 2])
        rstd = sb("rstd", [P, 2])
        minus_half = sb("minus_half", [P, 1])

        bank = [ctx.enter_context(nc.psum_tensor(f"att_bank{i}", [P, D], F32)) for i in range(8)]
        BANK_A, BANK_B, BANK_O, BANK_WO = 4, 5, 6, 7

        w_in = [sem(f"w_in{i}") for i in range(4)]
        w_hi_done, w_lo_done = sem("w_hi_done"), sem("w_lo_done")
        xt_in = [sem(f"xt_in{i}") for i in range(2)]
        x_in = [sem(f"x_in{i}") for i in range(UNROLL)]
        adj_in = [sem(f"adj_in{i}") for i in range(UNROLL)]
        x1_out = [sem(f"x1_out{i}") for i in range(UNROLL)]
        xt_hi_done, xt_lo_done = sem("xt_hi_done"), sem("xt_lo_done")
        bias_done = sem("bias_done")
        qk_ps = sem("qk_ps")
        qk_done = [sem("qk_even_done"), sem("qk_odd_done")]
        v_ps, v_done = sem("v_ps"), sem("v_done")
        s_ps, min_done, abs_done = sem("s_ps"), sem("min_done"), sem("abs_done")
        exp_done, inv_done, scale_done = sem("exp_done"), sem("inv_done"), sem("scale_done")
        probs_done, pt_ps = sem("probs_done"), sem("pt_ps")
        pt_even, pt_odd = sem("pt_even"), sem("pt_odd")
        pv_ps, o_hi_done, o_lo_done, wo_ps = sem("pv_ps"), sem("o_hi_done"), sem("o_lo_done"), sem("wo_ps")
        res_done, stats_done, mv_done, ve_done = sem("res_done"), sem("stats_done"), sem("mv_done"), sem("ve_done")
        rstd_done, x1_done = sem("rstd_done"), sem("x1_done")
        const_done = sem("const_done")
        minima_begun = sem("minima_begun")

        LAST = B - UNROLL

        def for_steps(eng, body):
            with eng.Fori(0, LAST // UNROLL) as i:
                for s in range(UNROLL):
                    body(i * UNROLL + s, s, i, False)
            for s in range(UNROLL):
                body(LAST + s, s, LAST // UNROLL, True)

        def exists(step, last, ahead):
            return not last or step + ahead < B

        block = ctx.enter_context(nc.Block())

        @block.sync
        def _(sp):
            def load_xt(g, p):
                sp.dma_start(xt_stage[:, p], io["x_t"][g]).then_inc(xt_in[p], 16)

            def load_w(n):
                sp.dma_start(w_stage[:, n % 2], io["w"][n]).then_inc(w_in[n], 16)

            load_xt(0, 0)
            load_w(Q)
            load_w(K)
            load_xt(1, 1)
            sp.dma_start(adj_nat[:, 0], io["adj"][0]).then_inc(adj_in[0], 16)
            for n in (V, O):
                sp.wait_ge(w_lo_done, n - 1)
                load_w(n)
            for s in range(1, UNROLL):
                sp.dma_start(adj_nat[:, s], io["adj"][s]).then_inc(adj_in[s], 16)
            for s in range(UNROLL):
                sp.dma_start(x_nat[:, s], io["x"][s]).then_inc(x_in[s], 16)

            def body(t, s, i, last):
                if s % 2 == 0 and not last:
                    g = i * 2 + s // 2
                    sp.wait_ge(xt_lo_done, g + 1)
                    load_xt(g + 2, s // 2)
                if exists(t, last, UNROLL):
                    sp.wait_ge(bias_done, t + 1)
                    sp.dma_start(adj_nat[:, s], io["adj"][t + UNROLL]).then_inc(adj_in[s], 16)
                    sp.wait_ge(res_done, t + 2)
                    sp.dma_start(x_nat[:, s], io["x"][t + UNROLL]).then_inc(x_in[s], 16)
                sp.wait_ge(x1_done, t + 1)
                sp.dma_start(x1_dram[t], x1[:, s]).then_inc(x1_out[s], 16)

            for_steps(sp, body)
            for s in range(UNROLL):
                sp.wait_ge(x1_out[s], 16 * (B // UNROLL + 1))

        @block.tensor
        def _(pe):
            def qk_unit(n, c, which, par, b):
                dst = bank[b][:, 0:GN]
                todo = [(w, x, k) for w, x in passes(W_hi, W_lo, xt_hi, xt_lo) for k in range(C)]
                for m, (w, x, k) in enumerate(todo):
                    mm = pe.matmul(dst, w[:, which, k, c * P:(c + 1) * P], x[:, par, k, :],
                                   start=m == 0, stop=m == len(todo) - 1)
                mm.then_inc(qk_ps, 1)

            def v_parts(s, b):
                par, j = (s // 2) % 2, s % 2
                todo = [(x, w, k) for x, w in passes(xt_hi, xt_lo, W_hi, W_lo) for k in range(C)]
                for m, (x, w, k) in enumerate(todo):
                    mm = pe.matmul(bank[b][:, :], x[:, par, k, j * P:(j + 1) * P], w[:, V, k, :],
                                   start=m == 0, stop=m == len(todo) - 1)
                    if m == len(todo) - 1:
                        mm.then_inc(v_ps, 1)
                    yield

            def scores(s):
                par, j = (s // 2) % 2, s % 2
                for c in range(C):
                    for r in range(HC):
                        rows = slice(r * HD, (r + 1) * HD)
                        mm = pe.matmul(bank[r][:, c * P:(c + 1) * P],
                                       qk[rows, par, Q, c, j * P:(j + 1) * P],
                                       qk[rows, par, K, c, j * P:(j + 1) * P], start=True, stop=True)
                mm.then_inc(s_ps, 1)

            for n in range(8):
                if n == 0:
                    pe.wait_ge(xt_lo_done, 1)
                if n % C == 0:
                    pe.wait_ge(w_lo_done, n // C + 1)
                if n >= 2:
                    pe.wait_ge(qk_done[n % 2], n // 2)
                qk_unit(n, n % C, n // C, 0, BANK_B - n % 2)
            pe.wait_ge(w_lo_done, 3)
            for s in range(2):
                pe.wait_ge(qk_done[s], 4)
                for _ in v_parts(s, BANK_B - s):
                    pass
            pe.wait_ge(xt_lo_done, 2)
            for n in range(8, AHEAD):
                if n < 10:
                    pe.wait_ge(v_done, n - 7)
                else:
                    pe.wait_ge(qk_done[n % 2], n // 2)
                qk_unit(n, n % C, Q, 1, BANK_B - n % 2)
            scores(0)
            pe.wait_ge(w_lo_done, 4)
            pe.wait_ge(const_done, 3)

            def body(t, s, i, last):
                def transposes(c):
                    pe.wait_ge(probs_done, 4 * t + c + 1)
                    for r in range(HC):
                        h = c * HC + r
                        mm = pe.transpose(bank[c][:, r * P:(r + 1) * P], probs[:, h * P:(h + 1) * P],
                                          ident[:, :])
                    mm.then_inc(pt_ps, 1)

                def weighted_values(c):
                    pe.wait_ge(pt_odd if c % 2 else pt_even, 2 * t + c // 2 + 1)
                    for r in range(HC):
                        h = c * HC + r
                        mm = pe.matmul(bank[BANK_O][r * HD:(r + 1) * HD, c * P:(c + 1) * P],
                                       v_sb[:, s, h * HD:(h + 1) * HD], probs_t[:, h * P:(h + 1) * P],
                                       start=True, stop=True)
                    if c == C - 1:
                        mm.then_inc(pv_ps, 1)

                def some_values(n):
                    for _ in range(n):
                        next(values, None)

                if exists(t, last, 2):
                    pe.wait_ge(res_done, t + 1)
                    values = v_parts((s + 2) % UNROLL, BANK_WO)
                else:
                    values = iter(())
                pe.wait_ge(v_done, t + 1)
                some_values(2)
                transposes(0)
                transposes(1)
                some_values(3)
                transposes(2)
                weighted_values(0)
                some_values(2)
                transposes(3)
                weighted_values(1)
                some_values(2)
                weighted_values(2)
                some_values(3)
                weighted_values(3)
                if exists(t, last, 1):
                    for done in qk_done:
                        pe.wait_ge(done, 2 * (t + 1 - (s + 1) % 2) + 4)
                    pe.wait_ge(pt_even, 2 * t + 2)
                    pe.wait_ge(pt_odd, 2 * t + 2)
                    scores((s + 1) % UNROLL)
                pe.wait_ge(o_lo_done, t + 1)
                if exists(t, last, 2):
                    pe.wait_ge(v_done, t + 3)
                else:
                    pe.wait_ge(res_done, t + 1)
                todo = [(a, w, k) for a, w in passes(o_hi, o_lo, W_hi, W_lo) for k in range(C)]
                for m, (a, w, k) in enumerate(todo):
                    mm = pe.matmul(bank[BANK_WO][:, :], a[:, k, :], w[:, O, k, :],
                                   start=m == 0, stop=m == len(todo) - 1)
                mm.then_inc(wo_ps, 1)
                if exists(t, last, 3):
                    ahead = s + 3
                    if s % 2:
                        pe.wait_ge(xt_lo_done, i * 2 + ahead // 2 + 1)
                    for k in range(UNITS):
                        pe.wait_ge(qk_done[k % 2], AHEAD // 2 + 2 * t + k // 2)
                        qk_unit(AHEAD + 4 * t + k, k, ahead % 2, (ahead // 2) % 2, BANK_B - k % 2)

            for_steps(pe, body)

        @block.scalar
        def _(act):
            def cut_w(n):
                act.wait_ge(w_in[n], 16)
                nc.scalar.activation(W_hi[:, n], w_stage[:, n % 2], ACT.Copy).then_inc(w_hi_done, 1)

            def copy_qk(n, c, which, par):
                act.wait_ge(qk_ps, n + 1)
                nc.scalar.activation(qk[:, par, which, c, :], bank[BANK_B][:, 0:GN], ACT.Copy,
                                     scale=-SCALE if which == Q else 1.0).then_inc(qk_done[0], 1)

            def exps(t, heads):
                for h in heads:
                    act.wait_ge(min_done, HEADS * t + h + 1)
                    nc.scalar.activation(probs[:, h * P:(h + 1) * P], neg_s[:, h * P:(h + 1) * P],
                                         ACT.Exp, bias=neg_max[:, h:h + 1], scale=-1.0,
                                         accum_out=row_sum[:, h:h + 1]).then_inc(exp_done, 1)

            def copy_v(t, s, b):
                act.wait_ge(v_ps, t + 1)
                nc.scalar.activation(v_sb[:, s, :], bank[b][:, :], ACT.Copy).then_inc(v_done, 1)

            cut_w(Q)
            cut_w(K)
            for n in range(8):
                if n == C:
                    act.wait_ge(w_lo_done, 1)
                    cut_w(V)
                if n % 2 == 0:
                    copy_qk(n, n % C, n // C, 0)
            cut_w(O)
            for s in range(2):
                copy_v(s, s, BANK_B - s)
            for n in range(8, AHEAD, 2):
                copy_qk(n, n % C, Q, 1)
            exps(0, range(HEADS))

            def body(t, s, i, last):
                for c in (1, 3):
                    act.wait_ge(pt_ps, 4 * t + c + 1)
                    nc.scalar.activation(probs_t[:, c * D:(c + 1) * D], bank[c][:, :],
                                         ACT.Copy).then_inc(pt_odd, 1)
                if exists(t, last, 2):
                    copy_v(t + 2, (s + 2) % UNROLL, BANK_WO)
                act.wait_ge(pv_ps, t + 1)
                nc.scalar.activation(o_hi[:, :, :], bank[BANK_O][:, :].rearrange("p (c n) -> p c n", c=C),
                                     ACT.Copy).then_inc(o_hi_done, 1)
                ahead = s + 3
                for k, heads in ((0, range(0, 8)), (2, range(8, 14)), (None, range(14, HEADS))):
                    if exists(t, last, 1):
                        exps(t + 1, heads)
                    if exists(t, last, 3) and k is not None:
                        copy_qk(AHEAD + 4 * t + k, k, ahead % 2, (ahead // 2) % 2)

            for_steps(act, body)

        @block.vector
        def _(dve):
            def cut_w(n):
                dve.wait_ge(w_hi_done, n + 1)
                nc.vector.tensor_tensor(W_lo[:, n], w_stage[:, n % 2], W_hi[:, n].bitcast(F32),
                                        ALU.subtract).then_inc(w_lo_done, 1)

            def cut_xt(g, p):
                dve.wait_ge(xt_in[p], 16)
                nc.vector.tensor_copy(xt_hi[:, p], xt_stage[:, p]).then_inc(xt_hi_done, 1)

            def copy_qk(n, c, which, par):
                dve.wait_ge(qk_ps, n + 1)
                nc.vector.tensor_scalar(qk[:, par, which, c, :], bank[BANK_A][:, 0:GN],
                                        -SCALE if which == Q else 1.0, None, ALU.mult).then_inc(qk_done[1], 1)

            def bias(t, s):
                dve.wait_ge(adj_in[s], (t - s) * 4 + 16)
                nc.vector.tensor_scalar(neg_bias[:, s % 2], adj_nat[:, s], -2.0, None,
                                        ALU.mult).then_inc(bias_done, 1)

            def minima(t, s):
                for h in range(HEADS):
                    c, r = h // HC, h % HC
                    nc.vector.tensor_tensor_reduce(neg_s[:, h * P:(h + 1) * P],
                                                   bank[r][:, c * P:(c + 1) * P], neg_bias[:, s % 2],
                                                   1.0, BIG, ALU.add, ALU.min,
                                                   neg_max[:, h:h + 1]).then_inc(min_done, 1)

            def largest(t, c):
                dve.wait_ge(min_done, HEADS * t + HC * (c + 1))
                heads = slice(c * HC, (c + 1) * HC)
                nc.vector.tensor_reduce(abs_max[:, heads],
                                        neg_s[:, c * D:(c + 1) * D].rearrange("p (h m) -> p h m", h=HC),
                                        AX_X, ALU.max, apply_absolute_value=True).then_inc(abs_done, 1)

            def inverse(t, c):
                heads = slice(c * HC, (c + 1) * HC)
                dve.wait_ge(exp_done, HEADS * t + HC * (c + 1))
                nc.vector.reciprocal(inv_sum[:, heads], row_sum[:, heads]).then_inc(inv_done, 1)

            def scales(t, c):
                heads = slice(c * HC, (c + 1) * HC)
                dve.wait_ge(inv_done, C * t + c + 1)
                dve.wait_ge(abs_done, C * t + c + 1)
                nc.vector.scalar_tensor_tensor(out=row_scale[:, heads], in0=abs_max[:, heads], scalar=0.0,
                                               in1=inv_sum[:, heads], op0=ALU.is_gt,
                                               op1=ALU.mult).then_inc(scale_done, 1)

            dve.sem_inc(res_done, 1)
            cut_xt(0, 0)
            cut_w(Q)
            cut_w(K)
            bias(0, 0)
            cut_xt(1, 1)
            for n in range(8):
                if n == C:
                    cut_w(V)
                if n % 2:
                    copy_qk(n, n % C, n // C, 0)
            cut_w(O)
            for n in range(9, AHEAD, 2):
                copy_qk(n, n % C, Q, 1)
            dve.wait_ge(s_ps, 1)
            dve.wait_ge(bias_done, 1)
            minima(0, 0)
            for c in range(C):
                largest(0, c)
            for c in range(C):
                inverse(0, c)
                scales(0, c)

            def body(t, s, i, last):
                more = exists(t, last, 1)
                for c in (0, 2):
                    dve.wait_ge(pt_ps, 4 * t + c + 1)
                    nc.vector.tensor_copy(probs_t[:, c * D:(c + 1) * D], bank[c][:, :]).then_inc(pt_even, 1)
                    if c == 0 and more:
                        bias(t + 1, (s + 1) % UNROLL)
                    if c == 0 and s % 2 and not last:
                        dve.wait_ge(v_ps, t + 1)
                        dve.wait_ge(xt_in[s // 2], i * 16 + 32)
                        nc.vector.tensor_copy(xt_hi[:, s // 2], xt_stage[:, s // 2]).then_inc(xt_hi_done, 1)
                dve.wait_ge(o_hi_done, t + 1)
                nc.vector.tensor_tensor(o_lo[:, :, :], bank[BANK_O][:, :].rearrange("p (c n) -> p c n", c=C),
                                        o_hi[:, :, :].bitcast(F32), ALU.subtract).then_inc(o_lo_done, 1)
                if more:
                    dve.wait_ge(s_ps, t + 2)
                    dve.wait_ge(bias_done, t + 2)
                    dve.sem_inc(minima_begun, 1)
                    minima(t + 1, s + 1)
                dve.wait_ge(wo_ps, t + 1)
                dve.wait_ge(x_in[s], i * 16 + 16)
                nc.vector.tensor_tensor(res[:, s % 2], bank[BANK_WO][:, :], x_nat[:, s],
                                        ALU.add).then_inc(res_done, 1)

                ahead = s + 3

                def copy_odd(k):
                    if exists(t, last, 3):
                        copy_qk(AHEAD + 4 * t + k, k, ahead % 2, (ahead // 2) % 2)

                if more:
                    largest(t + 1, 0)
                    inverse(t + 1, 0)
                dve.wait_ge(res_done, t + 2)
                nc.vector.bn_stats(stats[:, s % 2], res[:, s % 2]).then_inc(stats_done, 1)
                if more:
                    scales(t + 1, 0)
                    largest(t + 1, 1)
                dve.wait_ge(stats_done, t + 1)
                copy_odd(1)
                nc.vector.bn_aggr(mean_var[:, s % 2], stats[:, s % 2]).then_inc(mv_done, 1)
                if more:
                    inverse(t + 1, 1)
                    largest(t + 1, 2)
                    scales(t + 1, 1)
                    inverse(t + 1, 2)
                dve.wait_ge(mv_done, t + 1)
                nc.vector.tensor_scalar(var_eps[:, s % 2:s % 2 + 1], mean_var[:, s % 2, 1:2], EPS, None,
                                        ALU.add).then_inc(ve_done, 1)
                if more:
                    scales(t + 1, 2)
                    largest(t + 1, 3)
                    inverse(t + 1, 3)
                    scales(t + 1, 3)
                copy_odd(3)
                dve.wait_ge(rstd_done, t + 1)
                dve.wait_ge(x1_out[s], i * 16 + 16)
                nc.vector.tensor_scalar(x1[:, s], res[:, s % 2], mean_var[:, s % 2, 0:1],
                                        rstd[:, s % 2:s % 2 + 1], ALU.subtract,
                                        ALU.mult).then_inc(x1_done, 1)

            for_steps(dve, body)

        @block.gpsimd
        def _(pool):
            for s in range(UNROLL):
                pool.sem_inc(x1_out[s], 16)
            nc.gpsimd.memset(minus_half[:, :], -0.5).then_inc(const_done, 1)
            nc.gpsimd.memset(ident[:, :], 0.0).then_inc(const_done, 1)
            pool.wait_ge(const_done, 2)
            nc.gpsimd.affine_select(out=ident[:, :], in_=ident[:, :], compare_op=ALU.not_equal, fill=1.0,
                                    base=0, pattern=[[-1, P]], channel_multiplier=1).then_inc(const_done, 1)

            def xt_low(g, p):
                pool.wait_ge(xt_hi_done, g + 1)
                nc.gpsimd.tensor_tensor(xt_lo[:, p], xt_stage[:, p], xt_hi[:, p].bitcast(F32),
                                        ALU.subtract).then_inc(xt_lo_done, 1)

            def normalise(t, c):
                pool.wait_ge(scale_done, C * t + c + 1)
                part = probs[:, c * D:(c + 1) * D].rearrange("p (h m) -> p h m", h=HC)
                by = row_scale[:, c * HC:(c + 1) * HC].unsqueeze(2).to_broadcast([P, HC, P])
                nc.gpsimd.tensor_tensor(part, part, by, ALU.mult).then_inc(probs_done, 1)

            xt_low(0, 0)
            xt_low(1, 1)
            for c in range(C):
                normalise(0, c)

            def body(t, s, i, last):
                if s % 2 and not last:
                    xt_low(i * 2 + s // 2 + 2, s // 2)
                if exists(t, last, 1):
                    normalise(t + 1, 0)
                    normalise(t + 1, 1)
                pool.wait_ge(ve_done, t + 1)
                nc.gpsimd.tensor_tensor(rstd[:, s % 2:s % 2 + 1], var_eps[:, s % 2:s % 2 + 1],
                                        minus_half[:, :], ALU.pow).then_inc(rstd_done, 1)
                if exists(t, last, 1):
                    normalise(t + 1, 2)
                    normalise(t + 1, 3)

            for_steps(pool, body)


def expert_phase(nc, io, W_hi, W_lo, ones, expert_row, out_sum, out_sq, x1_dram, y_dram, B, D, E):
    C = D // P
    HALF = C // 2
    LAST = B - UNROLL
    with ExitStack() as ctx:
        def sb(name, shape, dt=F32):
            return ctx.enter_context(nc.sbuf_tensor(name, shape, dt))

        def sem(name):
            return ctx.enter_context(nc.semaphore(name))

        def y_of(s):
            both = ps_y[s % 2][:, :, 0:HALF * (P + 1)].rearrange("p b (c n) -> p b c n", c=HALF)
            return both[:, :, :, 0:P], both[:, :, :, P:P + 1]

        def halves_of(ring, s):
            return ring[:, s].rearrange("p (b c n) -> p b c n", b=2, c=HALF)

        e_stage = sb("e_stage", [P, 2, C, D])
        router_w = sb("router_w", [P, C, E])
        router_b = sb("router_b", [1, E])
        x1 = sb("g_x1", [P, UNROLL, D])
        adj_t = sb("adj_t", [P, UNROLL, P + 1])
        y_hi, y_lo = sb("y_hi", [P, UNROLL, D], F32R), sb("y_lo", [P, UNROLL, D], F32R)
        node_sum = sb("node_sum", [P, UNROLL, C])
        scores = sb("scores", [1, 8])
        best = sb("best", [1, 8])
        best_at = sb("best_at", [1, 8], U32)
        out = sb("g_out", [P, UNROLL, D])
        sq = sb("g_sq", [P, 2, D])
        ps_y = [ctx.enter_context(nc.psum_tensor(f"ps_y{i}", [P, 2, D], F32)) for i in range(2)]
        ps_scores = ctx.enter_context(nc.psum_tensor("ps_scores", [1, E], F32))
        ps_o = [ctx.enter_context(nc.psum_tensor(f"ps_o{i}", [P, D], F32)) for i in range(2)]

        e_in = [sem(f"e_in{i}") for i in range(4)]
        router_in = sem("router_in")
        e_hi_done, e_lo_done = sem("e_hi_done"), sem("e_lo_done")
        x1_in = [sem(f"g_x1_in{i}") for i in range(UNROLL)]
        adj_in = [sem(f"g_adj_in{i}") for i in range(UNROLL)]
        out_stored = [sem(f"out_stored{i}") for i in range(UNROLL)]
        y_ps, y_hi_done, y_lo_done = sem("y_ps"), sem("y_hi_done"), sem("y_lo_done")
        node_sum_done, scores_ps = sem("node_sum_done"), sem("scores_ps")
        scores_done, best_done, best_at_done = sem("scores_done"), sem("best_done"), sem("best_at_done")
        expert_done = sem("expert_done")
        route_go = sem("route_go")
        out_ps, out_done, sq_done = sem("out_ps"), sem("out_done"), sem("sq_done")
        filled, sum_done, sqsum_done = sem("filled"), sem("acc_sum_done"), sem("acc_sq_done")

        def for_steps(eng, body):
            with eng.Fori(0, LAST // UNROLL) as i:
                for s in range(UNROLL):
                    body(i * UNROLL + s, s, i, False)
            for s in range(UNROLL):
                body(LAST + s, s, LAST // UNROLL, True)

        def exists(step, last, ahead):
            return not last or step + ahead < B

        block = ctx.enter_context(nc.Block())

        @block.sync
        def _(sp):
            def load(t, s):
                sp.dma_start(x1[:, s], x1_dram[t]).then_inc(x1_in[s], 16)
                sp.dma_start(adj_t[:, s, 0:P], io["adj_t"][t]).then_inc(adj_in[s], 16)

            load(0, 0)
            load(1, 1)
            sp.dma_start(router_w[:, :, :], io["router_w"].rearrange("(c p) e -> p c e", p=P)).then_inc(router_in, 16)
            sp.dma_start(router_b[:, :], io["router_b"].unsqueeze(0)).then_inc(router_in, 16)
            for e in range(E):
                if e >= 2:
                    sp.wait_ge(e_lo_done, e - 1)
                sp.dma_start(e_stage[:, e % 2], io["expert_w"][e].rearrange("(c p) k -> p c k", p=P))\
                  .then_inc(e_in[e], 16)
            for s in range(2, UNROLL):
                load(s, s)

            def body(t, s, i, last):
                if exists(t, last, UNROLL):
                    sp.wait_ge(y_ps, t + 1)
                    load(t + UNROLL, s)
                sp.wait_ge(out_done, t + 3)
                sp.dma_start(y_dram[t], out[:, s]).then_inc(out_stored[s], 16)

            for_steps(sp, body)
            for s in range(UNROLL):
                sp.wait_ge(out_stored[s], 16 * (B // UNROLL + 1))

        @block.tensor
        def _(pe):
            def y_product(t, s, rnd):
                pe.wait_ge(x1_in[s], rnd * 16 + 16)
                pe.wait_ge(adj_in[s], rnd * 16 + 16)
                pe.wait_ge(y_lo_done, t + 1)
                for c in range(C):
                    dst = ps_y[s % 2][:, c // HALF, c % HALF * (P + 1):(c % HALF + 1) * (P + 1)]
                    mm = pe.matmul(dst, x1[:, s, c * P:(c + 1) * P], adj_t[:, s, :], start=True, stop=True)
                mm.then_inc(y_ps, 1)

            def router_scores(t, s):
                pe.wait_ge(node_sum_done, t + 1)
                pe.wait_ge(expert_done, t + 1)
                for c in range(C):
                    mm = pe.matmul(ps_scores[:, :], node_sum[:, s, c:c + 1], router_w[:, c, :],
                                   start=c == 0, stop=c == C - 1)
                mm.then_inc(scores_ps, 1)

            def out_product(t, s):
                p = s % 2
                e = pe.value_load(expert_row[0:1, bass.ds(t, 1)], min_val=0, max_val=E - 1)
                pe.wait_ge(y_lo_done, t + 3)
                pe.wait_ge(out_done, t + 1)
                todo = [(a, w, k) for a, w in passes(y_hi, y_lo, W_hi, W_lo) for k in range(C)]
                for m, (a, w, k) in enumerate(todo):
                    mm = pe.matmul(ps_o[p][:, :], a[:, s, k * P:(k + 1) * P],
                                   w[:, bass.ds(e, 1), k, :].rearrange("p a n -> p (a n)"),
                                   start=m == 0, stop=m == len(todo) - 1)
                mm.then_inc(out_ps, 1)

            pe.wait_ge(filled, 5)
            pe.wait_ge(router_in, 32)
            for s in range(2):
                y_product(s, s, 0)
                router_scores(s, s)
            pe.wait_ge(e_lo_done, E)

            def body(t, s, i, last):
                pe.wait_ge(expert_done, t + 2)
                if exists(t, last, 2):
                    y_product(t + 2, (s + 2) % UNROLL, i + (s + 2) // UNROLL)
                out_product(t, s)
                if exists(t, last, 2):
                    router_scores(t + 2, (s + 2) % UNROLL)

            for_steps(pe, body)

        @block.scalar
        def _(act):
            def y_high(t, s):
                act.wait_ge(y_ps, t + 1)
                nc.scalar.activation(halves_of(y_hi, s), y_of(s)[0], ACT.Copy).then_inc(y_hi_done, 1)

            y_high(0, 0)
            y_high(1, 1)
            for e in range(E):
                act.wait_ge(e_in[e], 16)
                nc.scalar.activation(W_hi[:, e], e_stage[:, e % 2], ACT.Copy).then_inc(e_hi_done, 1)

            def body(t, s, i, last):
                if exists(t, last, 2):
                    y_high(t + 2, (s + 2) % UNROLL)
                act.wait_ge(out_done, t + 3)
                act.wait_ge(sqsum_done, t + 1)
                nc.scalar.activation(sq[:, s % 2], out[:, s], ACT.Square).then_inc(sq_done, 1)

            for_steps(act, body)

        @block.vector
        def _(dve):
            def y_low(t, s):
                dve.wait_ge(y_hi_done, t + 1)
                nc.vector.tensor_copy(node_sum[:, s].rearrange("p (b c n) -> p b c n", b=2, n=1),
                                      y_of(s)[1]).then_inc(node_sum_done, 1)
                nc.vector.tensor_tensor(halves_of(y_lo, s), y_of(s)[0], halves_of(y_hi, s).bitcast(F32),
                                        ALU.subtract).then_inc(y_lo_done, 1)

            def route(t):
                dve.wait_ge(scores_ps, t + 1)
                nc.vector.scalar_tensor_tensor(out=scores[:, 0:E], in0=ps_scores[:, :], scalar=1.0 / P,
                                               in1=router_b[:, :], op0=ALU.mult,
                                               op1=ALU.add).then_inc(scores_done, 1)
                dve.wait_ge(scores_done, t + 1)
                dve.sem_inc(route_go, 1)
                nc.vector.max(best[:, :], scores[:, :]).then_inc(best_done, 1)
                dve.wait_ge(best_done, t + 1)
                dve.sem_inc(route_go, 1)
                nc.vector.max_index(best_at[:, :], best[:, :], scores[:, :]).then_inc(best_at_done, 1)
                dve.wait_ge(best_at_done, t + 1)
                nc.vector.tensor_copy(expert_row[:, bass.ds(t, 1)], best_at[:, 0:1]).then_inc(expert_done, 1)

            dve.sem_inc(expert_done, 1)
            dve.sem_inc(y_lo_done, 2)
            dve.sem_inc(out_done, 2)
            dve.wait_ge(filled, 5)
            dve.wait_ge(router_in, 32)
            for s in range(2):
                y_low(s, s)
                route(s)
            for e in range(E):
                dve.wait_ge(e_hi_done, e + 1)
                nc.vector.tensor_tensor(W_lo[:, e], e_stage[:, e % 2], W_hi[:, e].bitcast(F32),
                                        ALU.subtract).then_inc(e_lo_done, 1)

            def body(t, s, i, last):
                if exists(t, last, 2):
                    y_low(t + 2, (s + 2) % UNROLL)
                dve.wait_ge(out_ps, t + 1)
                dve.wait_ge(out_stored[s], i * 16 + 16)
                dve.wait_ge(sum_done, t + 1)
                nc.vector.tensor_copy(out[:, s], ps_o[s % 2][:, :]).then_inc(out_done, 1)
                if exists(t, last, 2):
                    route(t + 2)

            for_steps(dve, body)

        @block.gpsimd
        def _(pool):
            nc.gpsimd.memset(scores[:, :], -BIG).then_inc(filled, 1)
            nc.gpsimd.memset(ones[:, :], 1.0).then_inc(filled, 1)
            nc.gpsimd.memset(adj_t[:, :, P:P + 1], 1.0).then_inc(filled, 1)
            for s in range(UNROLL):
                pool.sem_inc(out_stored[s], 16)
            pool.sem_inc(sum_done, UNROLL)
            pool.sem_inc(sqsum_done, 2)
            nc.gpsimd.memset(out_sum[:, :, :], 0.0).then_inc(filled, 1)
            nc.gpsimd.memset(out_sq[:, :, :], 0.0).then_inc(filled, 1)
            pool.wait_ge(filled, 5)

            def body(t, s, i, last):
                pool.wait_ge(expert_done, t + 2)
                e = pool.value_load(expert_row[0:1, bass.ds(t, 1)], min_val=0, max_val=E - 1)
                pool.wait_ge(out_done, t + 3)
                pool.wait_ge(sum_done, t + UNROLL)
                acc = out_sum[:, bass.ds(e, 1), :].rearrange("p a n -> p (a n)")
                nc.gpsimd.tensor_tensor(acc, acc, out[:, s], ALU.add).then_inc(sum_done, 1)
                pool.wait_ge(sq_done, t + 1)
                pool.wait_ge(sqsum_done, t + 2)
                acc = out_sq[:, bass.ds(e, 1), :].rearrange("p a n -> p (a n)")
                nc.gpsimd.tensor_tensor(acc, acc, sq[:, s % 2], ALU.add).then_inc(sqsum_done, 1)

            for_steps(pool, body)


def norm_phase(nc, io, ident, ones, expert_row, out_sum, out_sq, x1_dram, y_dram, out_dram, B, D, E):
    C = D // P
    N = E * C
    RING = 8
    LAST = B - UNROLL
    with ExitStack() as ctx:
        def sb(name, shape, dt=F32):
            return ctx.enter_context(nc.sbuf_tensor(name, shape, dt))

        def sem(name):
            return ctx.enter_context(nc.semaphore(name))

        gamma, beta = sb("gamma", [P, N]), sb("beta", [P, N])
        expert_f, is_expert = sb("expert_f", [1, B]), sb("is_expert", [1, E, B])
        graphs = sb("graphs", [1, E])
        rows_of, inv_count = sb("rows_of", [P, E]), sb("inv_count", [P, E])
        mean, msq, mean2 = sb("bn_mean", [P, N]), sb("bn_msq", [P, N]), sb("bn_mean2", [P, N])
        var_eps, inv = sb("bn_var_eps", [P, N]), sb("bn_inv", [P, N])
        half_n, half_u = sb("half_n", [P, N]), sb("half_u", [P, UNROLL])
        mul_col, m_mul, add_col = sb("mul_col", [P, N]), sb("m_mul", [P, N]), sb("add_col", [P, N])
        diag = sb("diag", [P, 2, N, P])
        mul_row, add_row = sb("mul_row", [P, E, D]), sb("add_row", [P, E, D])
        y = sb("n_y", [P, RING, D])
        x1 = sb("n_x1", [P, RING, D])
        scaled = sb("scaled", [P, 2, D])
        shifted = sb("shifted", [P, 2, D])
        z = sb("n_z", [P, RING, D])
        outs = sb("n_out", [P, UNROLL, D])
        stats = sb("n_stats", [P, UNROLL, 6])
        m_diff, m_sum, v_sum = sb("m_diff", [P, UNROLL]), sb("m_sum", [P, UNROLL]), sb("v_sum", [P, UNROLL])
        m_diff2, v_eps = sb("m_diff2", [P, UNROLL]), sb("v_eps", [P, UNROLL])
        ve, nm = sb("n_ve", [P, 2, UNROLL]), sb("n_nm", [P, 2, UNROLL])
        rstd, nb = sb("n_rstd", [P, 2, UNROLL]), sb("n_nb", [P, 2, UNROLL])
        ps_cols = ctx.enter_context(nc.psum_tensor("ps_cols", [P, 2, N], F32))
        ps_count = ctx.enter_context(nc.psum_tensor("ps_count", [P, E], F32))
        ps_rows = [ctx.enter_context(nc.psum_tensor(f"ps_rows{i}", [P, D], F32)) for i in range(2)]

        gb_in, cols_ps, step, inv_done = sem("gb_in"), sem("cols_ps"), sem("bn_step"), sem("bn_inv_done")
        eq_done, count_ps = sem("eq_done"), sem("count_ps")
        halves, diag_done, rows_ps, rows_done = sem("halves"), sem("diag_done"), sem("rows_ps"), sem("rows_done")
        y_in = [sem(f"n_y_in{i}") for i in range(RING)]
        x1_in = [sem(f"n_x1_in{i}") for i in range(RING)]
        stored = [sem(f"stored{i}") for i in range(UNROLL)]
        scaled_done, shifted_done, z_done = sem("scaled_done"), sem("shifted_done"), sem("z_done")
        stats_done, mv_done, ve_done = sem("n_stats_done"), sem("n_mv_done"), sem("n_ve_done")
        rstd_done, nb_done, out_done = sem("n_rstd_done"), sem("nb_done"), sem("n_out_done")

        ROUNDS = B // RING

        def for_steps(eng, body):
            with eng.Fori(0, ROUNDS - 1) as i:
                for s in range(RING):
                    body(i * RING + s, s, i, False)
            for s in range(RING):
                body((ROUNDS - 1) * RING + s, s, ROUNDS - 1, True)

        block = ctx.enter_context(nc.Block())

        @block.sync
        def _(sp):
            sp.dma_start(gamma[:, :], io["gamma"]).then_inc(gb_in, 16)
            sp.dma_start(beta[:, :], io["beta"]).then_inc(gb_in, 16)

            def load(t, s):
                sp.dma_start(y[:, s], y_dram[t]).then_inc(y_in[s], 16)
                sp.dma_start(x1[:, s], x1_dram[t]).then_inc(x1_in[s], 16)

            for s in range(RING):
                load(s, s)

            def body(t, s, i, last):
                if not last:
                    sp.wait_ge(z_done, t + 1)
                    load(t + RING, s)

            for_steps(sp, body)

        @block.tensor
        def _(pe):
            for w, acc in enumerate((out_sum, out_sq)):
                for e in range(E):
                    for c in range(C):
                        mm = pe.matmul(ps_cols[:, w, e * C + c:e * C + c + 1], acc[:, e, c * P:(c + 1) * P],
                                       ones[:, 0:1], start=True, stop=True)
            mm.then_inc(cols_ps, 1)
            pe.wait_ge(step, 3)
            pe.matmul(ps_count[:, :], ones[0:1, :], graphs[:, :], start=True, stop=True).then_inc(count_ps, 1)
            for w in range(2):
                pe.wait_ge(diag_done, w + 1)
                for e in range(E):
                    n = w * E + e
                    if n >= 2:
                        pe.wait_ge(rows_done, n - 1)
                    for c in range(C):
                        mm = pe.matmul(ps_rows[n % 2][:, c * P:(c + 1) * P], ones[:, :],
                                       diag[:, w, e * C + c, :], start=True, stop=True)
                    mm.then_inc(rows_ps, 1)

        @block.vector
        def _(dve):
            count = [0]

            def chain(instruction):
                count[0] += 1
                instruction.then_inc(step, 1)
                dve.wait_ge(step, count[0])

            by_expert = "p (e c) -> p e c"
            over = inv_count[:, :].unsqueeze(2).to_broadcast([P, E, C])
            chain(nc.vector.tensor_copy(expert_f[:, :], expert_row[:, :]))
            for e in range(E):
                ins = nc.vector.tensor_scalar(is_expert[:, e, :], expert_f[:, :], float(e), None, ALU.is_equal)
                if e < E - 1:
                    ins.then_inc(eq_done, 1)
            dve.wait_ge(eq_done, E - 1)
            chain(ins)
            chain(nc.vector.tensor_reduce(graphs[:, :], is_expert[:, :, :], AX_X, ALU.add))
            dve.wait_ge(count_ps, 1)
            chain(nc.vector.tensor_scalar(rows_of[:, :], ps_count[:, :], float(P), 1.0, ALU.mult, ALU.max))
            chain(nc.vector.reciprocal(inv_count[:, :], rows_of[:, :]))
            dve.wait_ge(cols_ps, 1)
            chain(nc.vector.tensor_tensor(mean[:, :].rearrange(by_expert, e=E),
                                          ps_cols[:, 0, :].rearrange(by_expert, e=E), over, ALU.mult))
            chain(nc.vector.tensor_tensor(msq[:, :].rearrange(by_expert, e=E),
                                          ps_cols[:, 1, :].rearrange(by_expert, e=E), over, ALU.mult))
            chain(nc.vector.tensor_tensor(mean2[:, :], mean[:, :], mean[:, :], ALU.mult))
            chain(nc.vector.scalar_tensor_tensor(out=var_eps[:, :], in0=msq[:, :], scalar=EPS, in1=mean2[:, :],
                                                 op0=ALU.add, op1=ALU.subtract))
            dve.wait_ge(gb_in, 32)
            dve.wait_ge(inv_done, 1)
            chain(nc.vector.tensor_tensor(mul_col[:, :], inv[:, :], gamma[:, :], ALU.mult))
            chain(nc.vector.tensor_tensor(m_mul[:, :], mean[:, :], mul_col[:, :], ALU.mult))
            chain(nc.vector.tensor_tensor(add_col[:, :], beta[:, :], m_mul[:, :], ALU.subtract))
            for w, col in enumerate((mul_col, add_col)):
                for n in range(N):
                    ins = nc.vector.tensor_scalar(diag[:, w, n, :], ident[:, :], col[:, n:n + 1], None, ALU.mult)
                ins.then_inc(diag_done, 1)
            for w, row in enumerate((mul_row, add_row)):
                for e in range(E):
                    n = w * E + e
                    dve.wait_ge(rows_ps, n + 1)
                    nc.vector.tensor_copy(row[:, e, :], ps_rows[n % 2][:, :]).then_inc(rows_done, 1)
            dve.wait_ge(rows_done, 2 * E)

            def body(t, s, i, last):
                u = s // UNROLL
                e = dve.value_load(expert_row[0:1, bass.ds(t, 1)], min_val=0, max_val=E - 1)
                dve.wait_ge(scaled_done, t + 1)
                nc.vector.tensor_tensor(shifted[:, s % 2], scaled[:, s % 2],
                                        add_row[:, bass.ds(e, 1), :].rearrange("p a n -> p (a n)"),
                                        ALU.add).then_inc(shifted_done, 1)
                dve.wait_ge(shifted_done, t + 1)
                dve.wait_ge(x1_in[s], i * 16 + 16)
                dve.wait_ge(out_done, t + 1)
                nc.vector.scalar_tensor_tensor(out=z[:, s], in0=shifted[:, s % 2], scalar=0.0, in1=x1[:, s],
                                               op0=ALU.max, op1=ALU.add).then_inc(z_done, 1)
                dve.wait_ge(z_done, t + 1)
                nc.vector.bn_stats(stats[:, s % UNROLL], z[:, s]).then_inc(stats_done, 1)
                if s % UNROLL == UNROLL - 1:
                    r = i * 2 + u
                    dve.wait_ge(stats_done, t + 1)
                    nc.vector.tensor_tensor(m_diff[:, :], stats[:, :, 1], stats[:, :, 4],
                                            ALU.subtract).then_inc(mv_done, 1)
                    nc.vector.tensor_tensor(m_sum[:, :], stats[:, :, 1], stats[:, :, 4],
                                            ALU.add).then_inc(mv_done, 1)
                    nc.vector.tensor_tensor(v_sum[:, :], stats[:, :, 2], stats[:, :, 5],
                                            ALU.add).then_inc(mv_done, 1)
                    dve.wait_ge(mv_done, r * 5 + 3)
                    nc.vector.scalar_tensor_tensor(out=m_diff2[:, :], in0=m_diff[:, :], scalar=0.25,
                                                   in1=m_diff[:, :], op0=ALU.mult,
                                                   op1=ALU.mult).then_inc(mv_done, 1)
                    nc.vector.tensor_scalar(v_eps[:, :], v_sum[:, :], 1.0 / D, EPS, ALU.mult,
                                            ALU.add).then_inc(mv_done, 1)
                    nc.vector.tensor_scalar(nm[:, u, :], m_sum[:, :], -0.5, None, ALU.mult).then_inc(ve_done, 1)
                    dve.wait_ge(mv_done, r * 5 + 5)
                    nc.vector.tensor_tensor(ve[:, u, :], v_eps[:, :], m_diff2[:, :], ALU.add).then_inc(ve_done, 1)

            for_steps(dve, body)

        @block.gpsimd
        def _(pool):
            pool.sem_inc(out_done, RING)
            for s in range(UNROLL):
                pool.sem_inc(stored[s], 16)
            nc.gpsimd.memset(half_n[:, :], -0.5).then_inc(halves, 1)
            nc.gpsimd.memset(half_u[:, :], -0.5).then_inc(halves, 1)
            pool.wait_ge(halves, 2)
            pool.wait_ge(step, 9)
            nc.gpsimd.tensor_tensor(inv[:, :], var_eps[:, :], half_n[:, :], ALU.pow).then_inc(inv_done, 1)
            pool.wait_ge(rows_done, E)

            def body(t, s, i, last):
                e = pool.value_load(expert_row[0:1, bass.ds(t, 1)], min_val=0, max_val=E - 1)
                pool.wait_ge(y_in[s], i * 16 + 16)
                if s % UNROLL >= 2:
                    pool.wait_ge(shifted_done, t - 1)
                nc.gpsimd.tensor_tensor(scaled[:, s % 2], y[:, s],
                                        mul_row[:, bass.ds(e, 1), :].rearrange("p a n -> p (a n)"),
                                        ALU.mult).then_inc(scaled_done, 1)
                if s % UNROLL == UNROLL - 1:
                    u = s // UNROLL
                    r = i * 2 + u
                    pool.wait_ge(ve_done, r * 2 + 2)
                    nc.gpsimd.tensor_tensor(rstd[:, u, :], ve[:, u, :], half_u[:, :], ALU.pow).then_inc(rstd_done, 1)
                    pool.wait_ge(rstd_done, r + 1)
                    nc.gpsimd.tensor_tensor(nb[:, u, :], nm[:, u, :], rstd[:, u, :], ALU.mult).then_inc(nb_done, 1)

            for_steps(pool, body)

        @block.scalar
        def _(act):
            def body(t, s, i, last):
                u, k = s // UNROLL, s % UNROLL
                act.wait_ge(nb_done, i * 2 + u + 1)
                act.wait_ge(stored[k], (i * 2 + u) * 16 + 16)
                nc.scalar.activation(outs[:, k], z[:, s], ACT.Identity, bias=nb[:, u, k:k + 1],
                                     scale=rstd[:, u, k:k + 1]).then_inc(out_done, 1)
                act.wait_ge(out_done, t + RING + 1)
                act.dma_start(out_dram[t], outs[:, k]).then_inc(stored[k], 16)

            for_steps(act, body)
            for s in range(UNROLL):
                act.wait_ge(stored[s], 16 * (B // UNROLL + 1))


def build(nc, io, out_dram, B, D, E):
    C = D // P
    x1_dram = nc.dram_tensor("x1_scratch", [B, P, D], F32, kind="Internal").ap()
    y_dram = nc.dram_tensor("y_scratch", [B, P, D], F32, kind="Internal").ap()
    with ExitStack() as ctx:
        def sb(name, shape, dt=F32):
            return ctx.enter_context(nc.sbuf_tensor(name, shape, dt))

        ident = sb("ident", [P, P])
        ones = sb("ones", [P, P])
        expert_row = sb("expert_row", [1, B], U32)

        def cut_weights(phase, inner):
            hi = inner.enter_context(nc.sbuf_tensor(f"{phase}_hi", [P, 4, C, D], F32R))
            lo = inner.enter_context(nc.sbuf_tensor(f"{phase}_lo", [P, 4, C, D], F32R))
            return hi, lo

        with ExitStack() as inner:
            W_hi, W_lo = cut_weights("att_w", inner)
            attention_phase(nc, io, W_hi, W_lo, ident, x1_dram, B, D)
        out_sum, out_sq = sb("out_sum", [P, E, D]), sb("out_sq", [P, E, D])
        with ExitStack() as inner:
            W_hi, W_lo = cut_weights("exp_w", inner)
            expert_phase(nc, io, W_hi, W_lo, ones, expert_row, out_sum, out_sq, x1_dram, y_dram, B, D, E)
        norm_phase(nc, io, ident, ones, expert_row, out_sum, out_sq, x1_dram, y_dram, out_dram, B, D, E)


def kernel(x, adj, L0_gnn_Wq, L0_gnn_Wk, L0_gnn_Wv, L0_gnn_Wo, L1_gnn_router_w, L1_gnn_router_b,
           L1_gnn_expert_w, L1_gnn_bn_gamma, L1_gnn_bn_beta):
    import numpy as np
    import concourse.bacc as bacc
    from concourse.bass_utils import run_bass_kernel_spmd

    x, adj = np.asarray(x), np.asarray(adj)
    B, n, D = x.shape
    E = L1_gnn_expert_w.shape[0]
    C = D // P

    def features_first(w):
        return np.asarray(w).T.reshape(C, P, D).transpose(1, 0, 2)

    arrays = {
        "x": x,
        "x_t": x.reshape(B // GROUP, GROUP, n, C, P).transpose(0, 4, 3, 1, 2).reshape(B // GROUP, P, C, GROUP * n),
        "adj": adj,
        "adj_t": adj.transpose(0, 2, 1),
        "w": np.stack([features_first(w) for w in (L0_gnn_Wq, L0_gnn_Wk, L0_gnn_Wv, L0_gnn_Wo)]),
        "router_w": np.asarray(L1_gnn_router_w),
        "router_b": np.asarray(L1_gnn_router_b),
        "expert_w": np.asarray(L1_gnn_expert_w),
        "gamma": np.asarray(L1_gnn_bn_gamma).reshape(E * C, P).T,
        "beta": np.asarray(L1_gnn_bn_beta).reshape(E * C, P).T,
    }
    nc = bacc.Bacc("TRN2", target_bir_lowering=False, num_devices=1)
    io, maps = {}, {}
    for name, a in arrays.items():
        a = np.ascontiguousarray(a)
        maps[f"in_{name}"] = a
        io[name] = nc.dram_tensor(f"in_{name}", a.shape, mybir.dt.from_np(a.dtype), kind="ExternalInput").ap()
    out = nc.dram_tensor("out_x", [B, n, D], F32, kind="ExternalOutput").ap()
    build(nc, io, out, B, D, E)
    r = run_bass_kernel_spmd(nc, [maps], core_ids=[0])
    return r.results[0]["out_x"]
```

```python
from contextlib import ExitStack

import concourse.bass as bass
from concourse import mybir

F32 = mybir.dt.float32
F32R = mybir.dt.float32r
U32 = mybir.dt.uint32
ALU = mybir.AluOpType
ACT = mybir.ActivationFunctionType
AX_X = mybir.AxisListType.X

P = 128
HEADS = 16
EPS = 1e-5
BIG = 3.0e38
UNROLL = 4
KEPT_EVERY = UNROLL
GROUP = 2


def passes(hi_a, lo_a, hi_b, lo_b):
    return ((hi_a, hi_b), (hi_a, lo_b), (lo_a, hi_b))


def is_kept(s):
    return s % KEPT_EVERY == KEPT_EVERY - 2


def attention_phase(nc, io, W_hi, W_lo, w_stage, expert_w_in, ident, x1_dram, B, D):
    C = D // P
    HD = D // HEADS
    HC = P // HD
    SCALE = float(D) ** -0.5
    GN = GROUP * P
    UNITS = 2 * C // GROUP
    AHEAD = 12
    Q, K, V, O = range(4)

    with ExitStack() as ctx:
        def sb(name, shape, dt=F32):
            return ctx.enter_context(nc.sbuf_tensor(name, shape, dt))

        def sem(name):
            return ctx.enter_context(nc.semaphore(name))

        xt_stage = sb("xt_stage", [P, 2, C, GN])
        xt_hi = sb("xt_hi", [P, 2, C, GN], F32R)
        xt_lo = sb("xt_lo", [P, 2, C, GN], F32R)
        x_nat = sb("x_nat", [P, UNROLL, D])
        adj_nat = sb("adj_nat", [P, UNROLL, P])
        neg_bias = sb("neg_bias", [P, 2, P])
        qk = sb("qk", [P, 2, 2, C, GN])
        v_sb = sb("v_sb", [P, UNROLL, D])
        neg_s = sb("neg_s", [P, HEADS * P])
        probs = sb("probs", [P, HEADS * P])
        probs_t = sb("probs_t", [P, HEADS * P])
        o_hi = sb("o_hi", [P, C, P], F32R)
        o_lo = sb("o_lo", [P, C, P], F32R)
        res = sb("res", [P, 2, D])
        x1 = sb("x1", [P, UNROLL, D])
        neg_max = sb("neg_max", [P, HEADS])
        row_sum = sb("row_sum", [P, HEADS])
        abs_max = sb("abs_max", [P, HEADS])
        inv_sum = sb("inv_sum", [P, HEADS])
        row_scale = sb("row_scale", [P, HEADS])
        stats = sb("stats", [P, 2, 6])
        mean_var = sb("mean_var", [P, 2, 2])
        var_eps = sb("var_eps", [P, 2])
        rstd = sb("rstd", [P, 2])
        minus_half = sb("minus_half", [P, 1])

        bank = [ctx.enter_context(nc.psum_tensor(f"att_bank{i}", [P, D], F32)) for i in range(8)]
        BANK_A, BANK_B, BANK_O, BANK_WO = 4, 5, 6, 7

        w_in = [sem(f"w_in{i}") for i in range(4)]
        w_hi_done, w_lo_done = sem("w_hi_done"), sem("w_lo_done")
        xt_in = [sem(f"xt_in{i}") for i in range(2)]
        x_in = [sem(f"x_in{i}") for i in range(UNROLL)]
        adj_in = [sem(f"adj_in{i}") for i in range(UNROLL)]
        x1_out = [sem(f"x1_out{i}") for i in range(UNROLL)]
        xt_hi_done, xt_lo_done = sem("xt_hi_done"), sem("xt_lo_done")
        bias_done = sem("bias_done")
        qk_ps = sem("qk_ps")
        qk_done = [sem("qk_even_done"), sem("qk_odd_done")]
        v_ps, v_done = sem("v_ps"), sem("v_done")
        s_ps, min_done, abs_done = sem("s_ps"), sem("min_done"), sem("abs_done")
        exp_done, inv_done, scale_done = sem("exp_done"), sem("inv_done"), sem("scale_done")
        probs_done, pt_ps = sem("probs_done"), sem("pt_ps")
        pt_even, pt_odd = sem("pt_even"), sem("pt_odd")
        pv_ps, o_hi_done, o_lo_done, wo_ps = sem("pv_ps"), sem("o_hi_done"), sem("o_lo_done"), sem("wo_ps")
        res_done, stats_done, mv_done, ve_done = sem("res_done"), sem("stats_done"), sem("mv_done"), sem("ve_done")
        rstd_done, x1_done = sem("rstd_done"), sem("x1_done")
        const_done = sem("const_done")
        minima_begun = sem("minima_begun")

        LAST = B - UNROLL

        def for_steps(eng, body):
            with eng.Fori(0, LAST // UNROLL) as i:
                for s in range(UNROLL):
                    body(i * UNROLL + s, s, i, False)
            for s in range(UNROLL):
                body(LAST + s, s, LAST // UNROLL, True)

        def exists(step, last, ahead):
            return not last or step + ahead < B

        block = ctx.enter_context(nc.Block())

        @block.sync
        def _(sp):
            def load_xt(g, p):
                sp.dma_start(xt_stage[:, p], io["x_t"][g]).then_inc(xt_in[p], 16)

            def load_w(n):
                sp.dma_start(w_stage[:, n % 2], io["w"][n]).then_inc(w_in[n], 16)

            load_xt(0, 0)
            load_w(Q)
            load_w(K)
            load_xt(1, 1)
            sp.dma_start(adj_nat[:, 0], io["adj"][0]).then_inc(adj_in[0], 16)
            for n in (V, O):
                sp.wait_ge(w_lo_done, n - 1)
                load_w(n)
            for s in range(1, UNROLL):
                sp.dma_start(adj_nat[:, s], io["adj"][s]).then_inc(adj_in[s], 16)
            for s in range(UNROLL):
                sp.dma_start(x_nat[:, s], io["x"][s]).then_inc(x_in[s], 16)
            for e in range(2):
                sp.wait_ge(w_lo_done, V + e + 1)
                sp.dma_start(w_stage[:, e], io["expert_w"][e].rearrange("(c p) k -> p c k", p=P))\
                  .then_inc(expert_w_in[e], 16)

            def body(t, s, i, last):
                if s % 2 == 0 and not last:
                    g = i * 2 + s // 2
                    sp.wait_ge(xt_lo_done, g + 1)
                    load_xt(g + 2, s // 2)
                if exists(t, last, UNROLL):
                    sp.wait_ge(bias_done, t + 1)
                    sp.dma_start(adj_nat[:, s], io["adj"][t + UNROLL]).then_inc(adj_in[s], 16)
                    sp.wait_ge(res_done, t + 2)
                    sp.dma_start(x_nat[:, s], io["x"][t + UNROLL]).then_inc(x_in[s], 16)
                sp.wait_ge(x1_done, t + 1)
                sp.dma_start(x1_dram[t], x1[:, s]).then_inc(x1_out[s], 16)

            for_steps(sp, body)
            for s in range(UNROLL):
                sp.wait_ge(x1_out[s], 16 * (B // UNROLL + 1))

        @block.tensor
        def _(pe):
            def qk_unit(n, c, which, par, b):
                dst = bank[b][:, 0:GN]
                todo = [(w, x, k) for w, x in passes(W_hi, W_lo, xt_hi, xt_lo) for k in range(C)]
                for m, (w, x, k) in enumerate(todo):
                    mm = pe.matmul(dst, w[:, which, k, c * P:(c + 1) * P], x[:, par, k, :],
                                   start=m == 0, stop=m == len(todo) - 1)
                mm.then_inc(qk_ps, 1)

            def v_parts(s, b):
                par, j = (s // 2) % 2, s % 2
                todo = [(x, w, k) for x, w in passes(xt_hi, xt_lo, W_hi, W_lo) for k in range(C)]
                for m, (x, w, k) in enumerate(todo):
                    mm = pe.matmul(bank[b][:, :], x[:, par, k, j * P:(j + 1) * P], w[:, V, k, :],
                                   start=m == 0, stop=m == len(todo) - 1)
                    if m == len(todo) - 1:
                        mm.then_inc(v_ps, 1)
                    yield

            def scores(s, halfway=lambda: None):
                par, j = (s // 2) % 2, s % 2
                for c in range(C):
                    if c == C // 2:
                        halfway()
                    for r in range(HC):
                        rows = slice(r * HD, (r + 1) * HD)
                        mm = pe.matmul(bank[r][:, c * P:(c + 1) * P],
                                       qk[rows, par, Q, c, j * P:(j + 1) * P],
                                       qk[rows, par, K, c, j * P:(j + 1) * P], start=True, stop=True)
                mm.then_inc(s_ps, 1)

            for n in range(8):
                if n == 0:
                    pe.wait_ge(xt_lo_done, 1)
                if n % C == 0:
                    pe.wait_ge(w_lo_done, n // C + 1)
                if n >= 2:
                    pe.wait_ge(qk_done[n % 2], n // 2)
                qk_unit(n, n % C, n // C, 0, BANK_B - n % 2)
            for done in qk_done:
                pe.wait_ge(done, 4)
            scores(0)
            pe.wait_ge(w_lo_done, 3)
            for s in range(2):
                for _ in v_parts(s, BANK_B - s):
                    pass
            pe.wait_ge(xt_lo_done, 2)
            for n in range(8, AHEAD):
                if n < 10:
                    pe.wait_ge(v_done, n - 7)
                else:
                    pe.wait_ge(qk_done[n % 2], n // 2)
                qk_unit(n, n % C, Q, 1, BANK_B - n % 2)
            pe.wait_ge(const_done, 3)

            def body(t, s, i, last):
                def transposes(c):
                    pe.wait_ge(probs_done, 4 * t + c + 1)
                    for r in range(HC):
                        h = c * HC + r
                        mm = pe.transpose(bank[c][:, r * P:(r + 1) * P], probs[:, h * P:(h + 1) * P],
                                          ident[:, :])
                    mm.then_inc(pt_ps, 1)

                def weighted_values(c):
                    pe.wait_ge(pt_odd if c % 2 else pt_even, 2 * t + c // 2 + 1)
                    for r in range(HC):
                        h = c * HC + r
                        mm = pe.matmul(bank[BANK_O][r * HD:(r + 1) * HD, c * P:(c + 1) * P],
                                       v_sb[:, s, h * HD:(h + 1) * HD], probs_t[:, h * P:(h + 1) * P],
                                       start=True, stop=True)
                    if c == C - 1:
                        mm.then_inc(pv_ps, 1)

                def some_values(n):
                    for _ in range(n):
                        next(values, None)

                if exists(t, last, 2):
                    pe.wait_ge(res_done, t + 1)
                    values = v_parts((s + 2) % UNROLL, BANK_WO)
                else:
                    values = iter(())
                pe.wait_ge(v_done, t + 1)
                some_values(2)
                transposes(0)
                transposes(1)
                some_values(4)
                transposes(2)
                some_values(1)
                weighted_values(0)
                transposes(3)
                some_values(1)
                weighted_values(1)
                some_values(1)
                weighted_values(2)
                weighted_values(3)
                if exists(t, last, 1):
                    for done in qk_done:
                        pe.wait_ge(done, 2 * (t + 1 - (s + 1) % 2) + 4)
                    pe.wait_ge(pt_even, 2 * t + 2)
                    pe.wait_ge(pt_odd, 2 * t + 2)
                    scores((s + 1) % UNROLL, lambda: some_values(3))
                pe.wait_ge(w_lo_done, 4)
                pe.wait_ge(o_lo_done, t + 1)
                if exists(t, last, 2):
                    pe.wait_ge(v_done, t + 3)
                else:
                    pe.wait_ge(res_done, t + 1)
                todo = [(a, w, k) for a, w in passes(o_hi, o_lo, W_hi, W_lo) for k in range(C)]
                for m, (a, w, k) in enumerate(todo):
                    mm = pe.matmul(bank[BANK_WO][:, :], a[:, k, :], w[:, O, k, :],
                                   start=m == 0, stop=m == len(todo) - 1)
                mm.then_inc(wo_ps, 1)
                if exists(t, last, 3):
                    ahead = s + 3
                    if s % 2:
                        pe.wait_ge(xt_lo_done, i * 2 + ahead // 2 + 1)
                    for k in range(UNITS):
                        pe.wait_ge(qk_done[k % 2], AHEAD // 2 + 2 * t + k // 2)
                        qk_unit(AHEAD + 4 * t + k, k, ahead % 2, (ahead // 2) % 2, BANK_B - k % 2)

            for_steps(pe, body)

        @block.scalar
        def _(act):
            def cut_w(n):
                act.wait_ge(w_in[n], 16)
                nc.scalar.activation(W_hi[:, n], w_stage[:, n % 2], ACT.Copy).then_inc(w_hi_done, 1)

            def copy_qk(n, c, which, par):
                act.wait_ge(qk_ps, n + 1)
                nc.scalar.activation(qk[:, par, which, c, :], bank[BANK_B][:, 0:GN], ACT.Copy,
                                     scale=-SCALE if which == Q else 1.0).then_inc(qk_done[0], 1)

            def exps(t, heads):
                for h in heads:
                    act.wait_ge(min_done, HEADS * t + h + 1)
                    nc.scalar.activation(probs[:, h * P:(h + 1) * P], neg_s[:, h * P:(h + 1) * P],
                                         ACT.Exp, bias=neg_max[:, h:h + 1], scale=-1.0,
                                         accum_out=row_sum[:, h:h + 1]).then_inc(exp_done, 1)

            def copy_v(t, s, b):
                act.wait_ge(v_ps, t + 1)
                nc.scalar.activation(v_sb[:, s, :], bank[b][:, :], ACT.Copy).then_inc(v_done, 1)

            cut_w(Q)
            cut_w(K)
            for n in range(8):
                if n == C:
                    act.wait_ge(w_lo_done, 1)
                    cut_w(V)
                if n % 2 == 0:
                    copy_qk(n, n % C, n // C, 0)
            exps(0, range(0, 6))
            copy_v(0, 0, BANK_B)
            exps(0, range(6, 12))
            copy_v(1, 1, BANK_A)
            exps(0, range(12, HEADS))
            for n in range(8, AHEAD, 2):
                copy_qk(n, n % C, Q, 1)
            cut_w(O)

            def body(t, s, i, last):
                for c in (1, 3):
                    act.wait_ge(pt_ps, 4 * t + c + 1)
                    nc.scalar.activation(probs_t[:, c * D:(c + 1) * D], bank[c][:, :],
                                         ACT.Copy).then_inc(pt_odd, 1)
                act.wait_ge(pv_ps, t + 1)
                nc.scalar.activation(o_hi[:, :, :], bank[BANK_O][:, :].rearrange("p (c n) -> p c n", c=C),
                                     ACT.Copy).then_inc(o_hi_done, 1)
                if exists(t, last, 2):
                    copy_v(t + 2, (s + 2) % UNROLL, BANK_WO)
                ahead = s + 3
                for k, heads in ((0, range(0, 8)), (2, range(8, 14)), (None, range(14, HEADS))):
                    if exists(t, last, 1):
                        exps(t + 1, heads)
                    if exists(t, last, 3) and k is not None:
                        copy_qk(AHEAD + 4 * t + k, k, ahead % 2, (ahead // 2) % 2)

            for_steps(act, body)

        @block.vector
        def _(dve):
            def cut_w(n):
                dve.wait_ge(w_hi_done, n + 1)
                nc.vector.tensor_tensor(W_lo[:, n], w_stage[:, n % 2], W_hi[:, n].bitcast(F32),
                                        ALU.subtract).then_inc(w_lo_done, 1)

            def cut_xt(g, p):
                dve.wait_ge(xt_in[p], 16)
                nc.vector.tensor_copy(xt_hi[:, p], xt_stage[:, p]).then_inc(xt_hi_done, 1)

            def copy_qk(n, c, which, par):
                dve.wait_ge(qk_ps, n + 1)
                nc.vector.tensor_scalar(qk[:, par, which, c, :], bank[BANK_A][:, 0:GN],
                                        -SCALE if which == Q else 1.0, None, ALU.mult).then_inc(qk_done[1], 1)

            def bias(t, s):
                dve.wait_ge(adj_in[s], (t - s) * 4 + 16)
                nc.vector.tensor_scalar(neg_bias[:, s % 2], adj_nat[:, s], -2.0, None,
                                        ALU.mult).then_inc(bias_done, 1)

            def minima(t, s):
                for h in range(HEADS):
                    c, r = h // HC, h % HC
                    nc.vector.tensor_tensor_reduce(neg_s[:, h * P:(h + 1) * P],
                                                   bank[r][:, c * P:(c + 1) * P], neg_bias[:, s % 2],
                                                   1.0, BIG, ALU.add, ALU.min,
                                                   neg_max[:, h:h + 1]).then_inc(min_done, 1)

            def largest(t, c):
                dve.wait_ge(min_done, HEADS * t + HC * (c + 1))
                heads = slice(c * HC, (c + 1) * HC)
                nc.vector.tensor_reduce(abs_max[:, heads],
                                        neg_s[:, c * D:(c + 1) * D].rearrange("p (h m) -> p h m", h=HC),
                                        AX_X, ALU.max, apply_absolute_value=True).then_inc(abs_done, 1)

            def inverse(t, c):
                heads = slice(c * HC, (c + 1) * HC)
                dve.wait_ge(exp_done, HEADS * t + HC * (c + 1))
                nc.vector.reciprocal(inv_sum[:, heads], row_sum[:, heads]).then_inc(inv_done, 1)

            def scales(t, c):
                heads = slice(c * HC, (c + 1) * HC)
                dve.wait_ge(inv_done, C * t + c + 1)
                dve.wait_ge(abs_done, C * t + c + 1)
                nc.vector.scalar_tensor_tensor(out=row_scale[:, heads], in0=abs_max[:, heads], scalar=0.0,
                                               in1=inv_sum[:, heads], op0=ALU.is_gt,
                                               op1=ALU.mult).then_inc(scale_done, 1)

            dve.sem_inc(res_done, 1)
            cut_xt(0, 0)
            cut_w(Q)
            cut_w(K)
            bias(0, 0)
            cut_xt(1, 1)
            for n in range(8):
                if n == C:
                    cut_w(V)
                if n % 2:
                    copy_qk(n, n % C, n // C, 0)
            dve.wait_ge(s_ps, 1)
            dve.wait_ge(bias_done, 1)
            minima(0, 0)
            for c in range(C):
                largest(0, c)
                inverse(0, c)
                scales(0, c)
            for n in range(9, AHEAD - 1, 2):
                copy_qk(n, n % C, Q, 1)
            cut_w(O)

            def body(t, s, i, last):
                more = exists(t, last, 1)
                for c in (0, 2):
                    dve.wait_ge(pt_ps, 4 * t + c + 1)
                    nc.vector.tensor_copy(probs_t[:, c * D:(c + 1) * D], bank[c][:, :]).then_inc(pt_even, 1)
                    if c == 0 and exists(t, last, 2):
                        copy_qk(AHEAD + 4 * t - 1, C - 1, s % 2, ((s + 2) // 2) % 2)
                    if c == 0 and more:
                        bias(t + 1, (s + 1) % UNROLL)
                    if c == 0 and s % 2 and not last:
                        dve.wait_ge(v_ps, t + 1)
                        dve.wait_ge(xt_in[s // 2], i * 16 + 32)
                        nc.vector.tensor_copy(xt_hi[:, s // 2], xt_stage[:, s // 2]).then_inc(xt_hi_done, 1)
                dve.wait_ge(o_hi_done, t + 1)
                nc.vector.tensor_tensor(o_lo[:, :, :], bank[BANK_O][:, :].rearrange("p (c n) -> p c n", c=C),
                                        o_hi[:, :, :].bitcast(F32), ALU.subtract).then_inc(o_lo_done, 1)
                if more:
                    dve.wait_ge(s_ps, t + 2)
                    dve.wait_ge(bias_done, t + 2)
                    dve.sem_inc(minima_begun, 1)
                    minima(t + 1, s + 1)
                dve.wait_ge(wo_ps, t + 1)
                dve.wait_ge(x_in[s], i * 16 + 16)
                nc.vector.tensor_tensor(res[:, s % 2], bank[BANK_WO][:, :], x_nat[:, s],
                                        ALU.add).then_inc(res_done, 1)

                ahead = s + 3

                if more:
                    largest(t + 1, 0)
                    inverse(t + 1, 0)
                dve.wait_ge(res_done, t + 2)
                nc.vector.bn_stats(stats[:, s % 2], res[:, s % 2]).then_inc(stats_done, 1)
                if more:
                    scales(t + 1, 0)
                dve.wait_ge(stats_done, t + 1)
                if exists(t, last, 3):
                    copy_qk(AHEAD + 4 * t + 1, 1, ahead % 2, (ahead // 2) % 2)
                nc.vector.bn_aggr(mean_var[:, s % 2], stats[:, s % 2]).then_inc(mv_done, 1)
                if more:
                    inverse(t + 1, 1)
                    largest(t + 1, 1)
                    scales(t + 1, 1)
                    inverse(t + 1, 2)
                    largest(t + 1, 2)
                dve.wait_ge(mv_done, t + 1)
                nc.vector.tensor_scalar(var_eps[:, s % 2:s % 2 + 1], mean_var[:, s % 2, 1:2], EPS, None,
                                        ALU.add).then_inc(ve_done, 1)
                if more:
                    scales(t + 1, 2)
                    largest(t + 1, 3)
                    inverse(t + 1, 3)
                    scales(t + 1, 3)
                dve.wait_ge(rstd_done, t + 1)
                dve.wait_ge(x1_out[s], i * 16 + 16)
                nc.vector.tensor_scalar(x1[:, s], res[:, s % 2], mean_var[:, s % 2, 0:1],
                                        rstd[:, s % 2:s % 2 + 1], ALU.subtract,
                                        ALU.mult).then_inc(x1_done, 1)

            for_steps(dve, body)

        @block.gpsimd
        def _(pool):
            for s in range(UNROLL):
                pool.sem_inc(x1_out[s], 16)
            nc.gpsimd.memset(minus_half[:, :], -0.5).then_inc(const_done, 1)
            nc.gpsimd.memset(ident[:, :], 0.0).then_inc(const_done, 1)
            pool.wait_ge(const_done, 2)
            nc.gpsimd.affine_select(out=ident[:, :], in_=ident[:, :], compare_op=ALU.not_equal, fill=1.0,
                                    base=0, pattern=[[-1, P]], channel_multiplier=1).then_inc(const_done, 1)

            def xt_low(g, p):
                pool.wait_ge(xt_hi_done, g + 1)
                nc.gpsimd.tensor_tensor(xt_lo[:, p], xt_stage[:, p], xt_hi[:, p].bitcast(F32),
                                        ALU.subtract).then_inc(xt_lo_done, 1)

            def normalise(t, c):
                pool.wait_ge(scale_done, C * t + c + 1)
                part = probs[:, c * D:(c + 1) * D].rearrange("p (h m) -> p h m", h=HC)
                by = row_scale[:, c * HC:(c + 1) * HC].unsqueeze(2).to_broadcast([P, HC, P])
                nc.gpsimd.tensor_tensor(part, part, by, ALU.mult).then_inc(probs_done, 1)

            xt_low(0, 0)
            xt_low(1, 1)
            for c in range(C):
                normalise(0, c)

            def body(t, s, i, last):
                if s % 2 and not last:
                    xt_low(i * 2 + s // 2 + 2, s // 2)
                if exists(t, last, 1):
                    normalise(t + 1, 0)
                    normalise(t + 1, 1)
                pool.wait_ge(ve_done, t + 1)
                nc.gpsimd.tensor_tensor(rstd[:, s % 2:s % 2 + 1], var_eps[:, s % 2:s % 2 + 1],
                                        minus_half[:, :], ALU.pow).then_inc(rstd_done, 1)
                if exists(t, last, 1):
                    normalise(t + 1, 2)
                    normalise(t + 1, 3)

            for_steps(pool, body)


def expert_phase(nc, io, W_hi, W_lo, w_stage, expert_w_in, ones, expert_row, kept, out_sum, out_sq,
                 x1_dram, y_dram, B, D, E):
    C = D // P
    HALF = C // 2
    ROUNDS = 2
    with ExitStack() as ctx:
        def sb(name, shape, dt=F32):
            return ctx.enter_context(nc.sbuf_tensor(name, shape, dt))

        def sem(name):
            return ctx.enter_context(nc.semaphore(name))

        def y_of(s):
            both = ps_y[s % 2][:, :, 0:HALF * (P + 1)].rearrange("p b (c n) -> p b c n", c=HALF)
            return both[:, :, :, 0:P], both[:, :, :, P:P + 1]

        def halves_of(ring, s):
            return ring[:, s].rearrange("p (b c n) -> p b c n", b=2, c=HALF)

        staged = [w_stage[:, e] if e < 2 else kept[:, (e - 2) * C:(e - 1) * C] for e in range(E)]
        router_w = sb("router_w", [P, C, E])
        router_b = sb("router_b", [1, E])
        x1 = sb("g_x1", [P, UNROLL, D])
        adj_t = sb("adj_t", [P, UNROLL, P + 1])
        y_hi, y_lo = sb("y_hi", [P, UNROLL, D], F32R), sb("y_lo", [P, UNROLL, D], F32R)
        node_sum = sb("node_sum", [P, UNROLL, C])
        products = sb("products", [P, E, C])
        part_score = sb("part_score", [P, E])
        scores = sb("scores", [1, 8])
        best = sb("best", [1, 8])
        best_at = sb("best_at", [1, 8], U32)
        out = sb("g_out", [P, UNROLL, D])
        sq = sb("g_sq", [P, 2, D])
        ps_y = [ctx.enter_context(nc.psum_tensor(f"ps_y{i}", [P, 2, D], F32)) for i in range(2)]
        ps_scores = ctx.enter_context(nc.psum_tensor("ps_scores", [1, E], F32))
        ps_o = [ctx.enter_context(nc.psum_tensor(f"ps_o{i}", [P, D], F32)) for i in range(2)]

        router_in = sem("router_in")
        e_hi_done, e_lo_done = sem("e_hi_done"), sem("e_lo_done")
        x1_in = [sem(f"g_x1_in{i}") for i in range(UNROLL)]
        adj_in = [sem(f"g_adj_in{i}") for i in range(UNROLL)]
        out_stored = [sem(f"out_stored{i}") for i in range(UNROLL)]
        y_ps, y_hi_done, y_lo_done = sem("y_ps"), sem("y_hi_done"), sem("y_lo_done")
        products_done, part_done = sem("products_done"), sem("part_done")
        node_sum_done, scores_ps = sem("node_sum_done"), sem("scores_ps")
        scores_done, best_done, best_at_done = sem("scores_done"), sem("best_done"), sem("best_at_done")
        expert_done = sem("expert_done")
        route_go = sem("route_go")
        kept_done = sem("kept_done")
        out_ps, out_done, sq_done = sem("out_ps"), sem("out_done"), sem("sq_done")
        filled, sum_done, sqsum_done = sem("filled"), sem("acc_sum_done"), sem("acc_sq_done")

        def for_steps(eng, body):
            def rounds(i, last):
                for n in range(ROUNDS):
                    for s in range(UNROLL):
                        r = i * ROUNDS + n
                        body(r * UNROLL + s, s, r, last, (n, s) == (ROUNDS - 1, UNROLL - 1))

            with eng.Fori(0, B // (ROUNDS * UNROLL) - 1) as i:
                rounds(i, False)
            rounds(B // (ROUNDS * UNROLL) - 1, True)

        def exists(step, last, ahead):
            return not last or step + ahead < B

        block = ctx.enter_context(nc.Block())

        @block.sync
        def _(sp):
            def load(t, s):
                sp.dma_start(x1[:, s], x1_dram[t]).then_inc(x1_in[s], 16)
                sp.dma_start(adj_t[:, s, 0:P], io["adj_t"][t]).then_inc(adj_in[s], 16)

            load(0, 0)
            sp.dma_start(router_w[:, :, :], io["router_w"].rearrange("(c p) e -> p c e", p=P)).then_inc(router_in, 16)
            sp.dma_start(router_b[:, :], io["router_b"].unsqueeze(0)).then_inc(router_in, 16)
            load(1, 1)
            for e in range(2, E):
                sp.dma_start(staged[e], io["expert_w"][e].rearrange("(c p) k -> p c k", p=P))\
                  .then_inc(expert_w_in[e], 16)
            for s in range(2, UNROLL):
                load(s, s)

            def body(t, s, i, last, ends):
                if exists(t, last, UNROLL):
                    sp.wait_ge(y_ps, t + 1)
                    load(t + UNROLL, s)
                if not is_kept(s):
                    sp.wait_ge(out_done, t + 3)
                    sp.dma_start(y_dram[t], out[:, s]).then_inc(out_stored[s], 16)

            for_steps(sp, body)
            for s in range(UNROLL):
                if not is_kept(s):
                    sp.wait_ge(out_stored[s], 16 * (B // UNROLL + 1))

        @block.tensor
        def _(pe):
            def y_product(t, s, rnd):
                pe.wait_ge(x1_in[s], rnd * 16 + 16)
                pe.wait_ge(adj_in[s], rnd * 16 + 16)
                pe.wait_ge(y_lo_done, t + 1)
                for c in range(C):
                    dst = ps_y[s % 2][:, c // HALF, c % HALF * (P + 1):(c % HALF + 1) * (P + 1)]
                    mm = pe.matmul(dst, x1[:, s, c * P:(c + 1) * P], adj_t[:, s, :], start=True, stop=True)
                mm.then_inc(y_ps, 1)

            def router_scores(t, s):
                pe.wait_ge(part_done, t + 1)
                pe.wait_ge(expert_done, t + 1)
                pe.matmul(ps_scores[:, :], ones[:, 0:1], part_score[:, :],
                          start=True, stop=True).then_inc(scores_ps, 1)

            def load_expert(t):
                return pe.value_load(expert_row[0:1, bass.ds(t, 1)], min_val=0, max_val=E - 1)

            def out_product(t, s, e):
                p = s % 2
                pe.wait_ge(y_lo_done, t + 3)
                pe.wait_ge(out_done, t + 1)
                of_expert = [w[:, bass.ds(e, 1)].rearrange("p a c n -> p (a c) n") for w in (W_hi, W_lo)]
                todo = [(a, w, k) for a, w in passes(y_hi, y_lo, *of_expert) for k in range(C)]
                for m, (a, w, k) in enumerate(todo):
                    mm = pe.matmul(ps_o[p][:, :], a[:, s, k * P:(k + 1) * P], w[:, k, :],
                                   start=m == 0, stop=m == len(todo) - 1)
                mm.then_inc(out_ps, 1)

            pe.wait_ge(filled, 5)
            pe.wait_ge(router_in, 32)
            for s in range(2):
                y_product(s, s, 0)
                router_scores(s, s)
            pe.wait_ge(e_lo_done, E)

            loaded = []

            def body(t, s, i, last, ends):
                pe.wait_ge(expert_done, t + 2)
                if exists(t, last, 2):
                    y_product(t + 2, (s + 2) % UNROLL, i + (s + 2) // UNROLL)
                out_product(t, s, loaded.pop() if loaded else load_expert(t))
                if not ends:
                    pe.wait_ge(expert_done, t + 3)
                    loaded.append(load_expert(t + 1))
                if exists(t, last, 2):
                    router_scores(t + 2, (s + 2) % UNROLL)

            for_steps(pe, body)

        @block.scalar
        def _(act):
            def y_high(t, s):
                act.wait_ge(y_ps, t + 1)
                nc.scalar.activation(halves_of(y_hi, s), y_of(s)[0], ACT.Copy).then_inc(y_hi_done, 1)

            def cut_weights(e):
                act.wait_ge(expert_w_in[e], 16)
                nc.scalar.activation(W_hi[:, e], staged[e], ACT.Copy).then_inc(e_hi_done, 1)

            cut_weights(0)
            cut_weights(1)
            for s in range(2):
                y_high(s, s)
            for e in range(2, E):
                cut_weights(e)

            def body(t, s, i, last, ends):
                if exists(t, last, 2):
                    y_high(t + 2, (s + 2) % UNROLL)
                act.wait_ge(out_done, t + 3)
                act.wait_ge(sqsum_done, t + 1)
                nc.scalar.activation(sq[:, s % 2], out[:, s], ACT.Square).then_inc(sq_done, 1)

            for_steps(act, body)

        @block.vector
        def _(dve):
            def y_low(t, s):
                dve.wait_ge(y_hi_done, t + 1)
                nc.vector.tensor_copy(node_sum[:, s].rearrange("p (b c n) -> p b c n", b=2, n=1),
                                      y_of(s)[1]).then_inc(node_sum_done, 1)
                nc.vector.tensor_tensor(halves_of(y_lo, s), y_of(s)[0], halves_of(y_hi, s).bitcast(F32),
                                        ALU.subtract).then_inc(y_lo_done, 1)

            def part_scores(t, s):
                dve.wait_ge(node_sum_done, t + 1)
                nc.vector.tensor_tensor(products[:, :, :],
                                        node_sum[:, s, :].unsqueeze(1).to_broadcast([P, E, C]),
                                        router_w[:, :, :].rearrange("p c e -> p e c"),
                                        ALU.mult).then_inc(products_done, 1)
                dve.wait_ge(products_done, t + 1)
                nc.vector.tensor_reduce(part_score[:, :], products[:, :, :], AX_X, ALU.add).then_inc(part_done, 1)

            def route(t):
                dve.wait_ge(scores_ps, t + 1)
                nc.vector.scalar_tensor_tensor(out=scores[:, 0:E], in0=ps_scores[:, :], scalar=1.0 / P,
                                               in1=router_b[:, :], op0=ALU.mult,
                                               op1=ALU.add).then_inc(scores_done, 1)
                dve.wait_ge(scores_done, t + 1)
                dve.sem_inc(route_go, 1)
                nc.vector.max(best[:, :], scores[:, :]).then_inc(best_done, 1)
                dve.wait_ge(best_done, t + 1)
                dve.sem_inc(route_go, 1)
                nc.vector.max_index(best_at[:, :], best[:, :], scores[:, :]).then_inc(best_at_done, 1)
                dve.wait_ge(best_at_done, t + 1)
                nc.vector.tensor_copy(expert_row[:, bass.ds(t, 1)], best_at[:, 0:1]).then_inc(expert_done, 1)

            dve.sem_inc(expert_done, 1)
            dve.sem_inc(y_lo_done, 2)
            dve.sem_inc(out_done, 2)
            dve.sem_inc(kept_done, 1)

            def rest_of_weights(e):
                dve.wait_ge(e_hi_done, e + 1)
                nc.vector.tensor_tensor(W_lo[:, e], staged[e], W_hi[:, e].bitcast(F32),
                                        ALU.subtract).then_inc(e_lo_done, 1)

            rest_of_weights(0)
            rest_of_weights(1)
            dve.wait_ge(filled, 5)
            dve.wait_ge(router_in, 32)
            for s in range(2):
                y_low(s, s)
                part_scores(s, s)
                route(s)
            for e in range(2, E):
                rest_of_weights(e)

            def body(t, s, i, last, ends):
                if exists(t, last, 2):
                    y_low(t + 2, (s + 2) % UNROLL)
                    part_scores(t + 2, (s + 2) % UNROLL)
                if is_kept(s - 1):
                    dve.wait_ge(out_done, t + 2)
                    nc.vector.tensor_copy(kept[:, bass.ds(i, 1), :].rearrange("p a n -> p (a n)"),
                                          out[:, s - 1]).then_inc(kept_done, 1)
                dve.wait_ge(out_ps, t + 1)
                if is_kept(s):
                    dve.wait_ge(kept_done, i + 1)
                else:
                    dve.wait_ge(out_stored[s], i * 16 + 16)
                dve.wait_ge(sum_done, t + 1)
                nc.vector.tensor_copy(out[:, s], ps_o[s % 2][:, :]).then_inc(out_done, 1)
                if exists(t, last, 2):
                    route(t + 2)

            for_steps(dve, body)

        @block.gpsimd
        def _(pool):
            nc.gpsimd.memset(scores[:, :], -BIG).then_inc(filled, 1)
            nc.gpsimd.memset(ones[:, :], 1.0).then_inc(filled, 1)
            nc.gpsimd.memset(adj_t[:, :, P:P + 1], 1.0).then_inc(filled, 1)
            for s in range(UNROLL):
                pool.sem_inc(out_stored[s], 16)
            pool.sem_inc(sum_done, UNROLL)
            pool.sem_inc(sqsum_done, 2)
            nc.gpsimd.memset(out_sum[:, :, :], 0.0).then_inc(filled, 1)
            nc.gpsimd.memset(out_sq[:, :, :], 0.0).then_inc(filled, 1)
            pool.wait_ge(filled, 5)

            def body(t, s, i, last, ends):
                pool.wait_ge(expert_done, t + 2)
                e = pool.value_load(expert_row[0:1, bass.ds(t, 1)], min_val=0, max_val=E - 1)
                pool.wait_ge(out_done, t + 3)
                pool.wait_ge(sum_done, t + UNROLL)
                acc = out_sum[:, bass.ds(e, 1), :].rearrange("p a n -> p (a n)")
                nc.gpsimd.tensor_tensor(acc, acc, out[:, s], ALU.add).then_inc(sum_done, 1)
                pool.wait_ge(sq_done, t + 1)
                pool.wait_ge(sqsum_done, t + 2)
                acc = out_sq[:, bass.ds(e, 1), :].rearrange("p a n -> p (a n)")
                nc.gpsimd.tensor_tensor(acc, acc, sq[:, s % 2], ALU.add).then_inc(sqsum_done, 1)

            for_steps(pool, body)


def norm_phase(nc, io, ident, ones, expert_row, kept, out_sum, out_sq, x1_dram, y_dram, out_dram, B, D, E):
    C = D // P
    N = E * C
    RING = 8
    QUADS = RING // UNROLL
    with ExitStack() as ctx:
        def sb(name, shape, dt=F32):
            return ctx.enter_context(nc.sbuf_tensor(name, shape, dt))

        def sem(name):
            return ctx.enter_context(nc.semaphore(name))

        gamma, beta = sb("gamma", [P, N]), sb("beta", [P, N])
        expert_f, is_expert = sb("expert_f", [1, B]), sb("is_expert", [1, E, B])
        graphs = sb("graphs", [1, E])
        rows_of, inv_count = sb("rows_of", [P, E]), sb("inv_count", [P, E])
        mean, msq, mean2 = sb("bn_mean", [P, N]), sb("bn_msq", [P, N]), sb("bn_mean2", [P, N])
        var_eps, inv = sb("bn_var_eps", [P, N]), sb("bn_inv", [P, N])
        half_n, half_u = sb("half_n", [P, N]), sb("half_u", [P, UNROLL])
        mul_col, m_mul, add_col = sb("mul_col", [P, N]), sb("m_mul", [P, N]), sb("add_col", [P, N])
        diag = sb("diag", [P, 2, N, P])
        mul_row, add_row = sb("mul_row", [P, E, D]), sb("add_row", [P, E, D])
        y = sb("n_y", [P, RING, D])
        x1 = sb("n_x1", [P, RING, D])
        z = sb("n_z", [P, RING, D])
        outs = sb("n_out", [P, RING, D])
        stats = sb("n_stats", [P, UNROLL, 6])
        m_diff, m_sum, v_sum = sb("m_diff", [P, UNROLL]), sb("m_sum", [P, UNROLL]), sb("v_sum", [P, UNROLL])
        m_diff2, v_eps = sb("m_diff2", [P, UNROLL]), sb("v_eps", [P, UNROLL])
        ve, nm = sb("n_ve", [P, 2, UNROLL]), sb("n_nm", [P, 2, UNROLL])
        rstd, nb = sb("n_rstd", [P, 2, UNROLL]), sb("n_nb", [P, 2, UNROLL])
        ps_cols = ctx.enter_context(nc.psum_tensor("ps_cols", [P, 2, N], F32))
        ps_count = ctx.enter_context(nc.psum_tensor("ps_count", [P, E], F32))
        ps_rows = [ctx.enter_context(nc.psum_tensor(f"ps_rows{i}", [P, D], F32)) for i in range(2)]

        gb_in, cols_ps, step, inv_done = sem("gb_in"), sem("cols_ps"), sem("bn_step"), sem("bn_inv_done")
        eq_done, count_ps = sem("eq_done"), sem("count_ps")
        halves, diag_done, rows_ps, rows_done = sem("halves"), sem("diag_done"), sem("rows_ps"), sem("rows_done")
        y_in = [sem(f"n_y_in{i}") for i in range(RING)]
        x1_in = [sem(f"n_x1_in{i}") for i in range(RING)]
        stored = [sem(f"stored{i}") for i in range(RING)]
        scaled_done, shifted_done, z_done = sem("scaled_done"), sem("shifted_done"), sem("z_done")
        stats_done, mv_done, ve_done = sem("n_stats_done"), sem("n_mv_done"), sem("n_ve_done")
        rstd_done, nb_done, out_done = sem("n_rstd_done"), sem("nb_done"), sem("n_out_done")

        ROUNDS = B // RING

        def for_steps(eng, body):
            with eng.Fori(0, ROUNDS - 1) as i:
                for s in range(RING):
                    body(i * RING + s, s, i, False)
            for s in range(RING):
                body((ROUNDS - 1) * RING + s, s, ROUNDS - 1, True)

        block = ctx.enter_context(nc.Block())

        @block.sync
        def _(sp):
            sp.dma_start(gamma[:, :], io["gamma"]).then_inc(gb_in, 16)
            sp.dma_start(beta[:, :], io["beta"]).then_inc(gb_in, 16)

            def load(t, s):
                if not is_kept(s):
                    sp.dma_start(y[:, s], y_dram[t]).then_inc(y_in[s], 16)
                sp.dma_start(x1[:, s], x1_dram[t]).then_inc(x1_in[s], 16)

            for s in range(RING):
                load(s, s)

            def body(t, s, i, last):
                if not last:
                    sp.wait_ge(z_done, t + 1 + RING)
                    load(t + RING, s)

            for_steps(sp, body)

        @block.tensor
        def _(pe):
            for w, acc in enumerate((out_sum, out_sq)):
                for e in range(E):
                    for c in range(C):
                        mm = pe.matmul(ps_cols[:, w, e * C + c:e * C + c + 1], acc[:, e, c * P:(c + 1) * P],
                                       ones[:, 0:1], start=True, stop=True)
            mm.then_inc(cols_ps, 1)
            pe.wait_ge(step, 3)
            pe.matmul(ps_count[:, :], ones[0:1, :], graphs[:, :], start=True, stop=True).then_inc(count_ps, 1)
            for w in range(2):
                pe.wait_ge(diag_done, w + 1)
                for e in range(E):
                    n = w * E + e
                    if n >= 2:
                        pe.wait_ge(rows_done, n - 1)
                    for c in range(C):
                        mm = pe.matmul(ps_rows[n % 2][:, c * P:(c + 1) * P], ones[:, :],
                                       diag[:, w, e * C + c, :], start=True, stop=True)
                    mm.then_inc(rows_ps, 1)

        @block.vector
        def _(dve):
            count = [0]

            def chain(instruction):
                count[0] += 1
                instruction.then_inc(step, 1)
                dve.wait_ge(step, count[0])

            by_expert = "p (e c) -> p e c"
            over = inv_count[:, :].unsqueeze(2).to_broadcast([P, E, C])
            chain(nc.vector.tensor_copy(expert_f[:, :], expert_row[:, :]))
            for e in range(E):
                ins = nc.vector.tensor_scalar(is_expert[:, e, :], expert_f[:, :], float(e), None, ALU.is_equal)
                if e < E - 1:
                    ins.then_inc(eq_done, 1)
            dve.wait_ge(eq_done, E - 1)
            chain(ins)
            chain(nc.vector.tensor_reduce(graphs[:, :], is_expert[:, :, :], AX_X, ALU.add))
            dve.wait_ge(count_ps, 1)
            chain(nc.vector.tensor_scalar(rows_of[:, :], ps_count[:, :], float(P), 1.0, ALU.mult, ALU.max))
            chain(nc.vector.reciprocal(inv_count[:, :], rows_of[:, :]))
            dve.wait_ge(cols_ps, 1)
            chain(nc.vector.tensor_tensor(mean[:, :].rearrange(by_expert, e=E),
                                          ps_cols[:, 0, :].rearrange(by_expert, e=E), over, ALU.mult))
            chain(nc.vector.tensor_tensor(msq[:, :].rearrange(by_expert, e=E),
                                          ps_cols[:, 1, :].rearrange(by_expert, e=E), over, ALU.mult))
            chain(nc.vector.tensor_tensor(mean2[:, :], mean[:, :], mean[:, :], ALU.mult))
            chain(nc.vector.scalar_tensor_tensor(out=var_eps[:, :], in0=msq[:, :], scalar=EPS, in1=mean2[:, :],
                                                 op0=ALU.add, op1=ALU.subtract))
            dve.wait_ge(gb_in, 32)
            dve.wait_ge(inv_done, 1)
            chain(nc.vector.tensor_tensor(mul_col[:, :], inv[:, :], gamma[:, :], ALU.mult))
            chain(nc.vector.tensor_tensor(m_mul[:, :], mean[:, :], mul_col[:, :], ALU.mult))
            chain(nc.vector.tensor_tensor(add_col[:, :], beta[:, :], m_mul[:, :], ALU.subtract))
            for w, col in enumerate((mul_col, add_col)):
                nc.vector.tensor_tensor(diag[:, w], ident[:, :].unsqueeze(1).to_broadcast([P, N, P]),
                                        col[:, :].unsqueeze(2).to_broadcast([P, N, P]),
                                        ALU.mult).then_inc(diag_done, 1)
            for w, row in enumerate((mul_row, add_row)):
                for e in range(E):
                    n = w * E + e
                    dve.wait_ge(rows_ps, n + 1)
                    nc.vector.tensor_copy(row[:, e, :], ps_rows[n % 2][:, :]).then_inc(rows_done, 1)
            dve.wait_ge(rows_done, 2 * E)
            def load_expert(t):
                return dve.value_load(expert_row[0:1, bass.ds(t, 1)], min_val=0, max_val=E - 1)

            def shift(t, s, e):
                dve.wait_ge(scaled_done, t + 1)
                nc.vector.tensor_tensor(y[:, s], y[:, s],
                                        add_row[:, bass.ds(e, 1), :].rearrange("p a n -> p (a n)"),
                                        ALU.add).then_inc(shifted_done, 1)

            for s in range(2):
                shift(s, s, load_expert(s))

            def body(t, s, i, last):
                if s % 2 == 0:
                    return
                pair = ((t - 1, s - 1), (t, s))
                for n, place in pair:
                    dve.wait_ge(shifted_done, n + 1)
                    dve.wait_ge(x1_in[place], i * 16 + 16)
                    dve.wait_ge(out_done, n + 1)
                    nc.vector.scalar_tensor_tensor(out=z[:, place], in0=y[:, place], scalar=0.0,
                                                   in1=x1[:, place], op0=ALU.max,
                                                   op1=ALU.add).then_inc(z_done, 1)
                more = not last or s + 1 < RING
                if more:
                    first = load_expert(t + 1)
                for n, place in pair:
                    dve.wait_ge(z_done, n + 1 + RING)
                    nc.vector.bn_stats(stats[:, place % UNROLL], z[:, place]).then_inc(stats_done, 1)
                if more:
                    second = load_expert(t + 2)
                if s % UNROLL == UNROLL - 1:
                    u = s // UNROLL
                    r = i * QUADS + u
                    dve.wait_ge(stats_done, t + 1)
                    nc.vector.tensor_tensor(m_diff[:, :], stats[:, :, 1], stats[:, :, 4],
                                            ALU.subtract).then_inc(mv_done, 1)
                    nc.vector.tensor_tensor(m_sum[:, :], stats[:, :, 1], stats[:, :, 4],
                                            ALU.add).then_inc(mv_done, 1)
                    nc.vector.tensor_tensor(v_sum[:, :], stats[:, :, 2], stats[:, :, 5],
                                            ALU.add).then_inc(mv_done, 1)
                    dve.wait_ge(mv_done, r * 5 + 3)
                    nc.vector.scalar_tensor_tensor(out=m_diff2[:, :], in0=m_diff[:, :], scalar=0.25,
                                                   in1=m_diff[:, :], op0=ALU.mult,
                                                   op1=ALU.mult).then_inc(mv_done, 1)
                    nc.vector.tensor_scalar(v_eps[:, :], v_sum[:, :], 1.0 / D, EPS, ALU.mult,
                                            ALU.add).then_inc(mv_done, 1)
                    nc.vector.tensor_scalar(nm[:, u, :], m_sum[:, :], -0.5, None, ALU.mult).then_inc(ve_done, 1)
                    dve.wait_ge(mv_done, r * 5 + 5)
                    nc.vector.tensor_tensor(ve[:, u, :], v_eps[:, :], m_diff2[:, :], ALU.add).then_inc(ve_done, 1)
                if more:
                    shift(t + 1, (s + 1) % RING, first)
                    shift(t + 2, (s + 2) % RING, second)

            for_steps(dve, body)

        @block.gpsimd
        def _(pool):
            pool.sem_inc(out_done, RING)
            pool.sem_inc(z_done, RING)
            for s in range(RING):
                pool.sem_inc(stored[s], 16)
            nc.gpsimd.memset(half_n[:, :], -0.5).then_inc(halves, 1)
            nc.gpsimd.memset(half_u[:, :], -0.5).then_inc(halves, 1)
            pool.wait_ge(halves, 2)
            pool.wait_ge(step, 9)
            nc.gpsimd.tensor_tensor(inv[:, :], var_eps[:, :], half_n[:, :], ALU.pow).then_inc(inv_done, 1)
            pool.wait_ge(rows_done, E)

            def scale(t, s, i):
                e = pool.value_load(expert_row[0:1, bass.ds(t, 1)], min_val=0, max_val=E - 1)
                if is_kept(s):
                    pool.wait_ge(z_done, t + 1)
                    src = kept[:, bass.ds(i * QUADS + s // UNROLL, 1), :].rearrange("p a n -> p (a n)")
                else:
                    pool.wait_ge(y_in[s], i * 16 + 16)
                    src = y[:, s]
                nc.gpsimd.tensor_tensor(y[:, s], src,
                                        mul_row[:, bass.ds(e, 1), :].rearrange("p a n -> p (a n)"),
                                        ALU.mult).then_inc(scaled_done, 1)

            for s in range(UNROLL):
                scale(s, s, 0)

            def body(t, s, i, last):
                if not last or s + UNROLL < RING:
                    scale(t + UNROLL, (s + UNROLL) % RING, i + (s + UNROLL) // RING)
                if s % UNROLL == UNROLL - 1:
                    u = s // UNROLL
                    r = i * QUADS + u
                    pool.wait_ge(ve_done, r * 2 + 2)
                    nc.gpsimd.tensor_tensor(rstd[:, u, :], ve[:, u, :], half_u[:, :], ALU.pow).then_inc(rstd_done, 1)
                    pool.wait_ge(rstd_done, r + 1)
                    nc.gpsimd.tensor_tensor(nb[:, u, :], nm[:, u, :], rstd[:, u, :], ALU.mult).then_inc(nb_done, 1)

            for_steps(pool, body)

        @block.scalar
        def _(act):
            def body(t, s, i, last):
                u, k = s // UNROLL, s % UNROLL
                act.wait_ge(nb_done, i * QUADS + u + 1)
                act.wait_ge(stored[s], i * 16 + 16)
                nc.scalar.activation(outs[:, s], z[:, s], ACT.Identity, bias=nb[:, u, k:k + 1],
                                     scale=rstd[:, u, k:k + 1]).then_inc(out_done, 1)
                act.wait_ge(out_done, t + RING + 1)
                act.dma_start(out_dram[t], outs[:, s]).then_inc(stored[s], 16)

            for_steps(act, body)
            for s in range(RING):
                act.wait_ge(stored[s], 16 * (B // RING + 1))


def build(nc, io, out_dram, B, D, E):
    C = D // P
    x1_dram = nc.dram_tensor("x1_scratch", [B, P, D], F32, kind="Internal").ap()
    y_dram = nc.dram_tensor("y_scratch", [B, P, D], F32, kind="Internal").ap()
    with ExitStack() as ctx:
        def sb(name, shape, dt=F32):
            return ctx.enter_context(nc.sbuf_tensor(name, shape, dt))

        w_stage = sb("w_stage", [P, 2, C, D])
        expert_w_in = [ctx.enter_context(nc.semaphore(f"expert_w_in{e}")) for e in range(E)]
        ident = sb("ident", [P, P])
        ones = sb("ones", [P, P])
        expert_row = sb("expert_row", [1, B], U32)

        def cut_weights(phase, inner):
            hi = inner.enter_context(nc.sbuf_tensor(f"{phase}_hi", [P, 4, C, D], F32R))
            lo = inner.enter_context(nc.sbuf_tensor(f"{phase}_lo", [P, 4, C, D], F32R))
            return hi, lo

        with ExitStack() as inner:
            W_hi, W_lo = cut_weights("att_w", inner)
            attention_phase(nc, io, W_hi, W_lo, w_stage, expert_w_in, ident, x1_dram, B, D)
        kept = sb("kept", [P, B // KEPT_EVERY, D])
        out_sum, out_sq = sb("out_sum", [P, E, D]), sb("out_sq", [P, E, D])
        with ExitStack() as inner:
            W_hi, W_lo = cut_weights("exp_w", inner)
            expert_phase(nc, io, W_hi, W_lo, w_stage, expert_w_in, ones, expert_row, kept, out_sum, out_sq,
                         x1_dram, y_dram, B, D, E)
        norm_phase(nc, io, ident, ones, expert_row, kept, out_sum, out_sq, x1_dram, y_dram, out_dram, B, D, E)


def kernel(x, adj, L0_gnn_Wq, L0_gnn_Wk, L0_gnn_Wv, L0_gnn_Wo, L1_gnn_router_w, L1_gnn_router_b,
           L1_gnn_expert_w, L1_gnn_bn_gamma, L1_gnn_bn_beta):
    import numpy as np
    import concourse.bacc as bacc
    from concourse.bass_utils import run_bass_kernel_spmd

    x, adj = np.asarray(x), np.asarray(adj)
    B, n, D = x.shape
    E = L1_gnn_expert_w.shape[0]
    C = D // P

    def features_first(w):
        return np.asarray(w).T.reshape(C, P, D).transpose(1, 0, 2)

    arrays = {
        "x": x,
        "x_t": x.reshape(B // GROUP, GROUP, n, C, P).transpose(0, 4, 3, 1, 2).reshape(B // GROUP, P, C, GROUP * n),
        "adj": adj,
        "adj_t": adj.transpose(0, 2, 1),
        "w": np.stack([features_first(w) for w in (L0_gnn_Wq, L0_gnn_Wk, L0_gnn_Wv, L0_gnn_Wo)]),
        "router_w": np.asarray(L1_gnn_router_w),
        "router_b": np.asarray(L1_gnn_router_b),
        "expert_w": np.asarray(L1_gnn_expert_w),
        "gamma": np.asarray(L1_gnn_bn_gamma).reshape(E * C, P).T,
        "beta": np.asarray(L1_gnn_bn_beta).reshape(E * C, P).T,
    }
    nc = bacc.Bacc("TRN2", target_bir_lowering=False, num_devices=1)
    io, maps = {}, {}
    for name, a in arrays.items():
        a = np.ascontiguousarray(a)
        maps[f"in_{name}"] = a
        io[name] = nc.dram_tensor(f"in_{name}", a.shape, mybir.dt.from_np(a.dtype), kind="ExternalInput").ap()
    out = nc.dram_tensor("out_x", [B, n, D], F32, kind="ExternalOutput").ap()
    build(nc, io, out, B, D, E)
    r = run_bass_kernel_spmd(nc, [maps], core_ids=[0])
    return r.results[0]["out_x"]
```
